# Optimizing a Trainium2 kernel written in Bass

```python
import numpy as np
import jax
import jax.numpy as jnp

def _softmax(x, axis=-1):
    return jax.nn.softmax(x, axis=axis)

def _gelu(x):
    return jax.nn.gelu(x, approximate=True)

def _silu(x):
    return jax.nn.silu(x)

def _sigmoid(x):
    return jax.nn.sigmoid(x)

def _layernorm(x, axis=-1, eps=1e-05):
    m = jnp.mean(x, axis=axis, keepdims=True)
    v = jnp.var(x, axis=axis, keepdims=True)
    return (x - m) / jnp.sqrt(v + eps)

def _scatter_add(tgt, idx, src, axis=0):
    return tgt.at[idx].add(src)

def _segment_sum(src, seg, n):
    return jax.ops.segment_sum(src, seg, n)
kernel_name = 'mk_flamingo_gated_d1_seqx_r4_30e847'

def setup_inputs(seed: int=0):
    np.random.seed(seed)
    _w = jnp.asarray

    def _rec_inputs():
        import jax
        import jax.numpy as jnp
        _rk = jax.random.key(seed)
        x = -0.0002928 + 1 * jax.random.normal(jax.random.fold_in(_rk, 1), (4, 1024, 256), jnp.float32)
        _lenS = 1024 - jax.random.randint(jax.random.fold_in(_rk, 7), (4,), 0, max(1, 1024 // 4) + 1, jnp.int32)
        _lenS2 = 154 - jax.random.randint(jax.random.fold_in(_rk, 8), (4,), 0, max(1, 154 // 4) + 1, jnp.int32)
        _ctx_1024P = jax.random.normal(jax.random.fold_in(_rk, 11), (4, 16, 256), jnp.float32)
        _ctx_1024c = jax.random.dirichlet(jax.random.fold_in(_rk, 511), 0.3 * jnp.ones((16,), jnp.float32), (4, 154))
        _ctx_1024t = jnp.einsum('bsk,bkd->bsd', _ctx_1024c, _ctx_1024P)
        _ctx_1024t = _ctx_1024t * jax.lax.rsqrt(jnp.mean(jnp.square(_ctx_1024t)) + 1e-12) * 0.953939
        ctx_1024 = 2.81802e-05 + 1.00001 * (_ctx_1024t + 0.3 * jax.random.normal(jax.random.fold_in(_rk, 611), (4, 154, 256), jnp.float32))
        _g = jax.random.normal(jax.random.fold_in(_rk, 9001), (2, 1), jnp.float32)
        _g = jnp.sign(_g) * jnp.maximum(jnp.abs(_g), 1.0) + (_g == 0) * 1.0
        g_xattn = _g[0]
        g_ffn = _g[1]
        return (x, ctx_1024, g_xattn, g_ffn)
    x, ctx_1024, g_xattn, g_ffn = _rec_inputs()

    def _L0_xattn_setup():
        import jax, jax.numpy as jnp
        import numpy as np
        D_MODEL = 256
        N_HEADS = 16
        HEAD_DIM = D_MODEL // N_HEADS
        key = jax.random.key(seed)
        k1, k2, k3, k4, k5, k6 = jax.random.split(key, 6)
        B, T_q, T_kv = (4, 256, 1024)
        s = 1.0 / np.sqrt(D_MODEL)
        return {'query': jax.random.normal(k1, (B, T_q, D_MODEL), dtype=jnp.float32), 'kv_source': jax.random.normal(k2, (B, T_kv, D_MODEL), dtype=jnp.float32), 'w_q': jax.random.normal(k3, (D_MODEL, D_MODEL), dtype=jnp.float32) * s, 'w_k': jax.random.normal(k4, (D_MODEL, D_MODEL), dtype=jnp.float32) * s, 'w_v': jax.random.normal(k5, (D_MODEL, D_MODEL), dtype=jnp.float32) * s, 'w_o': jax.random.normal(k6, (D_MODEL, D_MODEL), dtype=jnp.float32) * s}
    _L0_xattn_all = _L0_xattn_setup()
    _L0_xattn_in = {k: v for k, v in _L0_xattn_all.items() if k in ('w_q', 'w_k', 'w_v', 'w_o')}
    del _L0_xattn_all

    def _L0_ffn_setup():
        import jax, jax.numpy as jnp
        import numpy as np
        B, S, D, E = (2, 512, 256, 8)
        key = jax.random.key(seed)
        ks = jax.random.split(key, 5)
        x = jax.random.normal(ks[0], (B, S, D), dtype=jnp.float32)
        router_w = jax.random.normal(ks[1], (E, D), dtype=jnp.float32) * 0.02
        router_b = jnp.zeros((E,), dtype=jnp.float32)
        expert_w = jax.random.normal(ks[2], (E, D, D), dtype=jnp.float32) * 0.02
        expert_b = jnp.zeros((E, D), dtype=jnp.float32)
        return {'x': x, 'router_w': router_w, 'router_b': router_b, 'expert_w': expert_w, 'expert_b': expert_b}
    _L0_ffn_all = _L0_ffn_setup()
    _L0_ffn_in = {k: v for k, v in _L0_ffn_all.items() if k in ('router_w', 'router_b', 'expert_w', 'expert_b')}
    del _L0_ffn_all
    return {'x': x, 'ctx_1024': ctx_1024, 'g_xattn': g_xattn, 'g_ffn': g_ffn, 'L0_xattn_w_q': _L0_xattn_in['w_q'], 'L0_xattn_w_k': _L0_xattn_in['w_k'], 'L0_xattn_w_v': _L0_xattn_in['w_v'], 'L0_xattn_w_o': _L0_xattn_in['w_o'], 'L0_ffn_router_w': _L0_ffn_in['router_w'], 'L0_ffn_router_b': _L0_ffn_in['router_b'], 'L0_ffn_expert_w': _L0_ffn_in['expert_w'], 'L0_ffn_expert_b': _L0_ffn_in['expert_b']}

def reference(x, ctx_1024, g_xattn, g_ffn, L0_xattn_w_q, L0_xattn_w_k, L0_xattn_w_v, L0_xattn_w_o, L0_ffn_router_w, L0_ffn_router_b, L0_ffn_expert_w, L0_ffn_expert_b):
    import jax
    import jax.numpy as jnp

    def _L0_xattn_ref(query, kv_source, w_q, w_k, w_v, w_o):
        import jax, jax.numpy as jnp
        import numpy as np
        D_MODEL = 256
        N_HEADS = 16
        HEAD_DIM = D_MODEL // N_HEADS
        B, T_q, _ = query.shape
        T_kv = kv_source.shape[1]
        q = (query @ w_q.T).reshape(B, T_q, N_HEADS, HEAD_DIM)
        k = (kv_source @ w_k.T).reshape(B, T_kv, N_HEADS, HEAD_DIM)
        v = (kv_source @ w_v.T).reshape(B, T_kv, N_HEADS, HEAD_DIM)
        scale = HEAD_DIM ** (-0.5)
        attn = jax.nn.softmax(jnp.einsum('bqhd,bkhd->bhqk', q, k) * scale, axis=-1)
        out = jnp.einsum('bhqk,bkhd->bqhd', attn, v).reshape(B, T_q, D_MODEL)
        return out @ w_o.T

    def _L0_ffn_ref(x, router_w, router_b, expert_w, expert_b):
        import jax, jax.numpy as jnp
        import numpy as np
        B, S, D, E = (2, 512, 256, 8)
        logits = jnp.einsum('bsd,ed->bse', x, router_w) + router_b
        probs = jax.nn.softmax(logits, axis=-1)
        weights = jnp.max(probs, axis=-1)
        top1 = jnp.argmax(probs, axis=-1)
        y_all = jnp.einsum('bsd,eod->bseo', x, expert_w) + expert_b
        y = jnp.take_along_axis(y_all, top1[:, :, None, None], axis=2)[:, :, 0, :]
        out = y * weights[:, :, None]
        return out
    x = x + jnp.tanh(g_xattn[0]) * _L0_xattn_ref(_layernorm(x, axis=-1), ctx_1024, L0_xattn_w_q, L0_xattn_w_k, L0_xattn_w_v, L0_xattn_w_o)
    x = x + jnp.tanh(g_ffn[0]) * _L0_ffn_ref(_layernorm(x, axis=-1), L0_ffn_router_w, L0_ffn_router_b, L0_ffn_expert_w, L0_ffn_expert_b)
    return x

_drawn_inputs = setup_inputs


def setup_inputs(seed=0):
    import zlib

    import numpy as np

    out = dict(_drawn_inputs(seed))
    spreads = {'L0_ffn_router_b': (0.0, 0.28), 'L0_ffn_expert_b': (0.0, 0.449)}
    factors = {}
    for name, (base, spread) in spreads.items():
        noise = np.random.default_rng([zlib.crc32(name.encode()), seed]).standard_normal(out[name].shape)
        drawn = base * np.exp(spread * noise) if base else spread * noise
        out[name] = jnp.asarray(drawn.astype(out[name].dtype))
    for name, factor in factors.items():
        out[name] = (out[name] * factor).astype(out[name].dtype)
    return out
```

```python
from contextlib import ExitStack

import concourse.bass as bass
from concourse import mybir

P = 128
ALU = mybir.AluOpType
ACT = mybir.ActivationFunctionType
F32 = mybir.dt.float32
BF16 = mybir.dt.bfloat16
AX_X = mybir.AxisListType.X
EPS = 1e-5


def gated_block(nc, x, ctx, g_xattn, g_ffn, w_q, w_k, w_v, w_o, router_w, router_b, expert_w, expert_b, out):
    B, S, D = x.shape
    KV = ctx.shape[1]
    E = router_w.shape[0]
    H = 16
    HD = D // H
    T = S // P
    C = D // P
    HPC = P // HD
    REM = KV - P
    KVP = P + 32
    HALF = 512
    NH = S // HALF
    TH = HALF // P
    SCALE = float(HD) ** -0.5
    PARTS = [(0, 0), (0, 1), (0, 2), (1, 0), (1, 1), (2, 0)]
    KROWS = len(PARTS) * HD + 1
    MROW = len(PARTS) * HD
    UNITS = [(hf, pr, par) for hf in range(NH) for pr in range(2) for par in range(2)]
    NU = len(UNITS)
    HEADS3 = [(0, 3), (3, 6), (6, 8)]

    with ExitStack() as es:
        def sb(name, shape, dt=F32):
            return es.enter_context(nc.sbuf_tensor(name, shape, dt))

        def sem(name):
            return es.enter_context(nc.semaphore(name))

        ident = sb("ident", [P, P])
        headmask = sb("headmask", [P, HPC], BF16)
        shared_a = sb("shared_a", [P, 2 * 5 * HALF])
        shared_b = sb("shared_b", [P, T * D])
        ewsb = shared_a[:, 0:E * C * D].rearrange("p (e c d) -> p e c d", e=E, c=C)
        probs = shared_a[:, :].rearrange("p (a k n) -> p a k n", a=2, k=5)
        wsb = shared_b[:, :].rearrange("p (e c d) -> p e c d", e=4, c=C)
        x1 = shared_b[:, :].rearrange("p (t d) -> p t d", t=T)
        wT = sb("wT", [P, 4, C, D])
        ewT = sb("ewT", [P, E, C, D])
        wop = sb("wop", [P, C, D])
        ctxT_rem = sb("ctxT_rem", [P, C, 4, 32])
        rwsb = sb("rwsb", [E, D])
        rwT = sb("rwT", [P, C, E])
        rb = sb("rb", [P, E])
        eb = sb("eb", [1, E, D])
        ones_row = sb("ones_row", [1, P])
        rev = sb("rev", [P, E])
        gates = sb("gates", [P, 2])
        tg = sb("tg", [P, 2])
        neg_half = sb("neg_half", [P, T])

        ctxA = sb("ctxA", [P, D])
        ctxB = sb("ctxB", [REM, D])
        ctxT = sb("ctxT", [P, C, KVP])
        kp = [sb(f"kp{i}", [P, C, KVP], BF16) for i in range(3)]
        rk = sb("rk", [P, C, KVP])
        kblock = sb("kblock", [P, C, HPC, KV], BF16)
        kstack_next = sb("kstack_next", [KROWS, H, KVP], BF16)
        kstack = sb("kstack", [KROWS, H, KVP], BF16)
        v_next = sb("v_next", [P, 2, 2, 4, 32])
        vr_next = sb("vr_next", [P, 2, 2, 4, 32])
        v_cur = sb("v_cur", [P, 2, 2, 4, 32])
        vr_cur = sb("vr_cur", [P, 2, 2, 4, 32])

        xt = sb("xt", [P, T, D])
        xn = sb("xn", [P, T, D])
        xnT = sb("xnT", [P, C, S])
        st6 = sb("st6", [P, 2, T, 6])
        mv = sb("mv", [P, 2, T, 2])
        ve = sb("ve", [P, 2, T])
        rs0 = sb("rs0", [P, 2, T])
        nt = sb("nt", [P, 2, T])
        rstd = sb("rstd", [P, 2, T])
        qp = [sb(f"qp{i}", [P, C, S], BF16) for i in range(3)]
        rq = sb("rq", [P, 2, HALF])
        qstack = sb("qstack", [KROWS, H, S], BF16)
        mx = sb("mx", [P, T, H])
        nmT = sb("nmT", [H, S], BF16)
        pv = sb("pv", [P, 2, HALF])
        den_pack = sb("den_pack", [P, 2, HALF // 32])
        rec_pack = sb("rec_pack", [P, 2, HALF // 32])
        rec_row = sb("rec_row", [P, 2, HALF])
        rec_b = sb("rec_b", [P, 2, HALF])
        pvn = sb("pvn", [P, 2, HALF])
        attnT = sb("attnT", [P, 2, S])

        xr = sb("xr", [P, T, D])
        xn2 = xn
        xn2T = xnT
        lg = sb("lg", [P, T, E])
        lm = sb("lm", [P, T])
        eq = sb("eq", [P, T, E])
        oh = sb("oh", [P, T, E])
        ex = sb("ex", [P, T, E])
        wt = sb("wt", [P, T])
        ybuf = sb("ybuf", [P, 2, D])
        ob = xr

        bank = [es.enter_context(nc.psum_tensor(f"bank{i}", [P, 512], F32)) for i in range(8)]
        FB, AB, SB_, OB = bank[0:2], bank[2:4], bank[4:6], bank[6:8]

        f_full = [sem(f"f_full{i}") for i in range(2)]
        f_free = [sem(f"f_free{i}") for i in range(2)]
        a_full = [sem(f"a_full{i}") for i in range(2)]
        a_free = [sem(f"a_free{i}") for i in range(2)]
        s_full = [sem(f"s_full{i}") for i in range(2)]
        o_full = [sem(f"o_full{i}") for i in range(2)]
        o_free = [sem(f"o_free{i}") for i in range(2)]
        weights_in = sem("weights_in")
        small_in = sem("small_in")
        experts_in = sem("experts_in")
        pool_consts = sem("pool_consts")
        stats_seen = sem("stats_seen")
        rec_seen = sem("rec_seen")
        wop_half = sem("wop_half")
        wop_done = sem("wop_done")
        tanh_done = sem("tanh_done")
        headmask_done = sem("headmask_done")
        wT_done = [sem("wT_done_even"), sem("wT_done_odd")]
        ctx_in = sem("ctx_in")
        x_in = sem("x_in")
        xr_in = sem("xr_in")
        ctxT_done = sem("ctxT_done")
        k1_done = sem("k1_done")
        k_parts = sem("k_parts")
        kblock_done = sem("kblock_done")
        kstack_in = sem("kstack_in")
        kv_cur = sem("kv_cur")
        v_done = sem("v_done")
        var_done = sem("var_done")
        rs0_done = sem("rs0_done")
        xn_done = sem("xn_done")
        xnT_done = sem("xnT_done")
        q1_done = sem("q1_done")
        rq_done = sem("rq_done")
        q2_done = sem("q2_done")
        q3_done = sem("q3_done")
        qstack_in = [[sem(f"qstack_in{c}{h}") for h in range(NH)] for c in range(C)]
        mx_done = sem("mx_done")
        nmT_done = sem("nmT_done")
        m_in = [sem(f"m_in{h}") for h in range(NH)]
        probs_done = sem("probs_done")
        pv_out = sem("pv_out")
        den_in = sem("den_in")
        rec_done = sem("rec_done")
        rec_in = sem("rec_in")
        pvn_done = sem("pvn_done")
        attn_done = sem("attn_done")
        x1_done = sem("x1_done")
        var2_done = sem("var2_done")
        rs02_done = sem("rs02_done")
        xn2_done = sem("xn2_done")
        xn2T_done = sem("xn2T_done")
        lg_done = sem("lg_done")
        ex_done = sem("ex_done")
        out_done = sem("out_done")
        out_written = sem("out_written")
        dve_chain = sem("dve_chain")
        pool_chain = sem("pool_chain")

        block = es.enter_context(nc.Block())

        NW = 4 + E
        SETUP_F = [NW // 2 + 1, NW // 2]
        UF = [13, 13]
        UA = [40, 40]
        K_DVE = 127
        K_POOL = 60
        US = 20
        UO = 4

        def f_use(i, b, n):
            return SETUP_F[i] + b * UF[i] + n

        def link(eng, chain, counter, base, ins):
            counter[0] += 1
            ins.then_inc(chain, 1)
            eng.wait_ge(chain, base + counter[0])

        def counts(n):
            return not (isinstance(n, int) and n <= 0)

        def value(eng, n):
            return n if isinstance(n, int) else eng.to_reg(n)

        def tok(ap, start):
            return ap.rearrange("b s d -> (b s d)")[bass.ds(start, S * D)].rearrange("(p t d) -> p t d", p=P, d=D)

        @block.sync
        def _(sp):
            for i, w in enumerate((w_k, w_v, w_q, w_o)):
                sp.dma_start(wsb[:, i], w.rearrange("(c p) d -> p c d", p=P)).then_inc(weights_in, 16)
            sp.dma_start(rwsb[:, :], router_w).then_inc(small_in, 16)
            sp.dma_start(rb[:, :], router_b.rearrange("(a e) -> a e", a=1).broadcast_to([P, E])).then_inc(small_in, 16)
            sp.dma_start(gates[:, 0:1], g_xattn.rearrange("(a e) -> a e", a=1).broadcast_to([P, 1])).then_inc(small_in, 16)
            sp.dma_start(gates[:, 1:2], g_ffn.rearrange("(a e) -> a e", a=1).broadcast_to([P, 1])).then_inc(small_in, 16)
            sp.dma_start(eb[:, :, :], expert_b.rearrange("(a e) d -> a e d", a=1)).then_inc(small_in, 16)
            sp.dma_start(ewsb[:, :, :, :], expert_w.rearrange("e (c p) d -> p e c d", p=P)).then_inc(experts_in, 16)

            def batch(b):
                x_at, ctx_at, ctx_rem_at = b * (S * D), b * (KV * D), b * (KV * D) + P * D
                if not isinstance(b, int):
                    x_at, ctx_at, ctx_rem_at = sp.snap(x_at), sp.snap(ctx_at), sp.snap(ctx_rem_at)
                ctx_flat = ctx.rearrange("b s d -> (b s d)")
                n_0 = value(sp, b)
                if counts(n_0):
                    sp.wait_ge(ctxT_done, n_0)
                sp.dma_start(ctxA[:, :], ctx_flat[bass.ds(ctx_at, P * D)].rearrange("(p d) -> p d", d=D)).then_inc(ctx_in, 16)
                sp.dma_start(ctxB[:, :], ctx_flat[bass.ds(ctx_rem_at, REM * D)].rearrange("(p d) -> p d", d=D)).then_inc(ctx_in, 16)
                n_0 = value(sp, b * T)
                if counts(n_0):
                    sp.wait_ge(xn_done, n_0)
                sp.dma_start(xt[:, :, :], tok(x, x_at)).then_inc(x_in, 16)
                n_0 = value(sp, (b + 1) * 2)
                n_1 = value(sp, b + 1)
                n_2 = value(sp, b)
                sp.wait_ge(k_parts, n_0)
                sp.wait_ge(k1_done, n_1)
                if counts(n_2):
                    sp.wait_ge(kv_cur, n_2)
                for n, (_, kpart) in enumerate(PARTS):
                    for c in range(C):
                        sp.dma_start(kstack_next[n * HD:(n + 1) * HD, c * HPC:(c + 1) * HPC, :],
                                     kp[kpart][:, c, :]).then_inc(kstack_in, 16)
                for hf in range(NH):
                    for c in range(C):
                        n_0 = value(sp, b * US)
                        n_1 = value(sp, b * US)
                        n_2 = value(sp, b * 4 + hf * 2 + c + 1)
                        n_3 = value(sp, b * 4 + hf * 2 + c + 1)
                        n_4 = value(sp, b * 4 + hf * 2 + c + 1)
                        if counts(n_0):
                            sp.wait_ge(s_full[0], n_0)
                        if counts(n_1):
                            sp.wait_ge(s_full[1], n_1)
                        sp.wait_ge(q1_done, n_2)
                        sp.wait_ge(q2_done, n_3)
                        sp.wait_ge(q3_done, n_4)
                        for n, (qpart, _) in enumerate(PARTS):
                            sp.dma_start(qstack[n * HD:(n + 1) * HD, c * HPC:(c + 1) * HPC, hf * HALF:(hf + 1) * HALF],
                                         qp[qpart][:, c, hf * HALF:(hf + 1) * HALF]
                                         ).then_inc(qstack_in[c][hf], 16)
                for hf in range(NH):
                    n_0 = value(sp, b * NH + hf + 1)
                    sp.wait_ge(nmT_done, n_0)
                    sp.dma_start(qstack[MROW:MROW + 1, :, hf * HALF:(hf + 1) * HALF],
                                 nmT[:, hf * HALF:(hf + 1) * HALF]).then_inc(m_in[hf], 16)
                n_0 = value(sp, 16 * b)
                if counts(n_0):
                    sp.wait_ge(out_written, n_0)
                sp.dma_start(xr[:, :, :], tok(x, x_at)).then_inc(xr_in, 16)
                for u, (hf, pr, par) in enumerate(UNITS):
                    row = 16 * (1 - par)
                    n_0 = value(sp, b * NU + u + 1)
                    sp.wait_ge(pv_out, n_0)
                    sp.dma_start(den_pack[:, u % 2, :],
                                 pv[row:P:32, u % 2, :].rearrange("j (i k) -> j i k", k=HALF // 32)).then_inc(den_in, 16)
                    n_0 = value(sp, b * NU + u + 1)
                    sp.wait_ge(rec_done, n_0)
                    sp.dma_start(rec_row[row:P:32, u % 2, :].rearrange("j (i k) -> j i k", k=HALF // 32),
                                 rec_pack[:, u % 2, :]).then_inc(rec_in, 16)
                n_0 = value(sp, (b + 1) * T)
                sp.wait_ge(out_done, n_0)
                sp.dma_start(tok(out, x_at), ob[:, :, :]).then_inc(out_written, 16)

            batch(0)
            with sp.Fori(1, B) as b:
                batch(b)
            sp.wait_ge(out_written, 16 * B)

        @block.tensor
        def _(pe):
            pe.wait_ge(pool_consts, 1)
            for i in range(NW):
                if i == 0:
                    pe.wait_ge(weights_in, 64)
                if i == 3:
                    pe.wait_ge(wop_done, 1)
                if i == 4:
                    pe.wait_ge(experts_in, 16)
                if i >= 2:
                    pe.wait_ge(f_free[i % 2], i // 2)
                for kc in range(C):
                    for oc in range(C):
                        dst = FB[i % 2][:, (kc * C + oc) * P:(kc * C + oc + 1) * P]
                        if i == 3:
                            src = wop[:, oc, kc * P:(kc + 1) * P]
                        elif i < 4:
                            src = wsb[:, i, oc, kc * P:(kc + 1) * P]
                        else:
                            src = ewsb[:, i - 4, oc, kc * P:(kc + 1) * P]
                        mm = pe.transpose(dst, src, ident[:, :])
                mm.then_inc(f_full[i % 2], 1)
            pe.wait_ge(small_in, 80)
            pe.wait_ge(f_free[0], NW // 2)
            for kc in range(C):
                mm = pe.transpose(FB[0][:, kc * E:(kc + 1) * E], rwsb[:, kc * P:(kc + 1) * P], ident[0:E, 0:E])
            mm.then_inc(f_full[0], 1)
            pe.wait_ge(wT_done[0], NW // 2 + 1)
            pe.wait_ge(wT_done[1], NW // 2)

            def batch(b):
                used = [0, 0]

                def f_begin(i):
                    if counts(f_use(i, b, used[i])):
                        pe.wait_ge(f_free[i], f_use(i, b, used[i]))
                    used[i] += 1
                    return FB[i]

                pe.wait_ge(ctx_in, 32 * (b + 1))
                F = f_begin(0)
                for kc in range(C):
                    pe.transpose(F[:, kc * KV:kc * KV + P], ctxA[:, kc * P:(kc + 1) * P], ident[:, :])
                    mm = pe.transpose(F[:, kc * KV + P:(kc + 1) * KV], ctxB[:, kc * P:(kc + 1) * P], ident[0:REM, 0:REM])
                mm.then_inc(f_full[0], 1)
                pe.wait_ge(ctxT_done, b + 1)
                F = f_begin(1)
                for c in range(C):
                    for kc in range(C):
                        mm = pe.matmul(F[:, c * KVP:(c + 1) * KVP], wT[:, 0, kc, c * P:(c + 1) * P], ctxT[:, kc, :],
                                       start=kc == 0, stop=kc == C - 1)
                mm.then_inc(f_full[1], 1)
                F = f_begin(0)
                for kc in range(C):
                    pe.matmul(F[:, 0:D], ctxT[:, kc, 0:P], wT[:, 1, kc, :], start=kc == 0, stop=kc == C - 1)
                for kc in range(C):
                    mm = pe.matmul(F[:, D:2 * D], ctxT_rem[:, kc].rearrange("p j k -> p (j k)"), wT[:, 1, kc, :],
                                   start=kc == 0, stop=kc == C - 1)
                mm.then_inc(f_full[0], 1)
                for hf in range(NH):
                    for c in range(C):
                        F = f_begin((c + 1) % 2)
                        for t in range(TH):
                            if c == 0:
                                pe.wait_ge(xn_done, b * T + hf * TH + t + 1)
                            mm = pe.transpose(F[:, t * P:(t + 1) * P], xn[:, hf * TH + t, c * P:(c + 1) * P], ident[:, :])
                        mm.then_inc(f_full[(c + 1) % 2], 1)
                for hf in range(NH):
                    pe.wait_ge(xnT_done, b * 4 + 2 * hf + 2)
                    for c in range(C):
                        F = f_begin((c + 1) % 2)
                        for kc in range(C):
                            mm = pe.matmul(F[:, :], wT[:, 2, kc, c * P:(c + 1) * P], xnT[:, kc, hf * HALF:(hf + 1) * HALF],
                                           start=kc == 0, stop=kc == C - 1)
                        mm.then_inc(f_full[(c + 1) % 2], 1)
                pe.wait_ge(kblock_done, b + 1)
                n = 0
                for hf in range(NH):
                    for t in range(hf * TH, (hf + 1) * TH):
                        for c in range(C):
                            if t % TH == 0:
                                pe.wait_ge(q1_done, b * 4 + 2 * hf + c + 1)
                            for lo, hi in HEADS3:
                                i = n % 2
                                if counts(b * UA[i] + n // 2):
                                    pe.wait_ge(a_free[i], b * UA[i] + n // 2)
                                pe.matmul(AB[i][:, 0:(hi - lo) * KV], qp[0][:, c, t * P:(t + 1) * P],
                                          kblock[:, c, lo:hi, :], start=True, stop=True).then_inc(a_full[i], 1)
                                n += 1
                    pe.wait_ge(mx_done, b * NH + hf + 1)
                    i = 1 - hf
                    F = f_begin(i)
                    for t in range(TH):
                        mm = pe.transpose(F[0:H, t * P:(t + 1) * P], mx[:, hf * TH + t, :], ident[:, :])
                    mm.then_inc(f_full[i], 1)
                pe.wait_ge(kstack_in, (b + 1) * 16 * 12)
                pe.wait_ge(kv_cur, b + 1)

                def scores(u):
                    hf, pr, par = UNITS[u]
                    if par == 0:
                        pe.wait_ge(qstack_in[pr][hf], (b + 1) * 16 * len(PARTS))
                    if pr == 0 and par == 0:
                        pe.wait_ge(m_in[hf], (b + 1) * 16)
                    h0 = pr * 8 + par * 4
                    for k in range(5):
                        m = 5 * u + k
                        if m >= 2:
                            if counts(b * 5 * NU + m - 1):
                                pe.wait_ge(probs_done, b * 5 * NU + m - 1)
                        else:
                            if counts(b * 5 * NU):
                                pe.wait_ge(probs_done, b * 5 * NU)
                        bk = SB_[m % 2]
                        if k < 4:
                            mm = pe.matmul(bk[:, :], kstack[:, h0 + k, 0:P], qstack[:, h0 + k, hf * HALF:(hf + 1) * HALF],
                                           start=True, stop=True)
                        else:
                            for j in range(4):
                                mm = pe.matmul(bk[32 * j:32 * j + 32, :], kstack[:, h0 + j, P:KVP],
                                               qstack[:, h0 + j, hf * HALF:(hf + 1) * HALF], start=True, stop=True)
                        mm.then_inc(s_full[m % 2], 1)

                def weighted(u):
                    hf, pr, par = UNITS[u]
                    o = OB[u % 2]
                    if counts(b * UO + u // 2):
                        pe.wait_ge(o_free[u % 2], b * UO + u // 2)
                    pe.wait_ge(probs_done, b * 5 * NU + 5 * u + 5)
                    for j in range(4):
                        pe.matmul(o[32 * j:32 * j + 32, :], v_cur[:, pr, par, j, :], probs[:, u % 2, j, :],
                                  start=True, stop=False, skip_group_check=True)
                    pe.matmul(o[:, :], vr_cur[:, pr, par, :, :], probs[:, u % 2, 4, :],
                              start=False, stop=True, skip_group_check=True).then_inc(o_full[u % 2], 1)

                def oproj(hf):
                    pe.wait_ge(attn_done, b * 4 + 2 * hf + 2)
                    for t in range(hf * TH, (hf + 1) * TH):
                        i = (t + 1) % 2
                        F = f_begin(i)
                        for pr in range(2):
                            mm = pe.matmul(F[:, 0:D], attnT[:, pr, t * P:(t + 1) * P], wT[:, 3, pr, :],
                                           start=pr == 0, stop=pr == 1)
                        mm.then_inc(f_full[i], 1)

                for u in range(NU):
                    scores(u)
                    if u >= 1:
                        weighted(u - 1)
                weighted(NU - 1)
                for hf in range(NH):
                    oproj(hf)
                for tp in range(T // 2):
                    i = (tp + 1) % 2
                    F = f_begin(i)
                    pe.wait_ge(xn2_done, b * T + 2 * tp + 2)
                    for c in range(C):
                        for t in range(2):
                            mm = pe.transpose(F[:, (c * 2 + t) * P:(c * 2 + t + 1) * P], xn2[:, 2 * tp + t, c * P:(c + 1) * P],
                                              ident[:, :])
                    mm.then_inc(f_full[i], 1)
                F = f_begin(1)
                pe.wait_ge(xn2T_done, b * 4 + 4)
                for t in range(T):
                    for kc in range(C):
                        mm = pe.matmul(F[:, t * E:(t + 1) * E], xn2T[:, kc, t * P:(t + 1) * P], rwT[:, kc, :],
                                       start=kc == 0, stop=kc == C - 1)
                mm.then_inc(f_full[1], 1)
                for t in range(T):
                    for e2 in range(E // 2):
                        i = n % 2
                        if counts(b * UA[i] + n // 2):
                            pe.wait_ge(a_free[i], b * UA[i] + n // 2)
                        for s in range(2):
                            e = 2 * e2 + s
                            pe.matmul(AB[i][:, s * D:(s + 1) * D], ones_row[:, :], eb[:, e, :], start=True, stop=False)
                            for kc in range(C):
                                mm = pe.matmul(AB[i][:, s * D:(s + 1) * D], xn2T[:, kc, t * P:(t + 1) * P],
                                               ewT[:, e, kc, :], start=False, stop=kc == C - 1)
                        mm.then_inc(a_full[i], 1)
                        n += 1
                assert used == UF and n == UA[0] * 2, (used, n)

            batch(0)
            with pe.Fori(1, B) as b:
                batch(b)

        @block.scalar
        def _(act):
            act.wait_ge(small_in, 80)
            act.activation(tg[:, :], gates[:, :], ACT.Tanh).then_inc(tanh_done, 1)
            for i in range(0, NW, 2):
                act.wait_ge(f_full[0], i // 2 + 1)
                dst = wT[:, i] if i < 4 else ewT[:, i - 4]
                src = FB[0][:, :]
                if i in (0, 2):
                    src = src.rearrange("p (g h d) -> p g d h", h=HPC, d=HD)
                    act.copy(dst.rearrange("p c (g d h) -> p (c g) d h", h=HPC, d=HD), src).then_inc(f_free[0], 1)
                else:
                    act.copy(dst.rearrange("p c d -> p (c d)"), src).then_inc(f_free[0], 1)
                act.wait_ge(f_free[0], i // 2 + 1)
                act.sem_inc(wT_done[0], 1)
            act.wait_ge(f_full[0], NW // 2 + 1)
            act.copy(rwT[:, :, :].rearrange("p c e -> p (c e)"), FB[0][:, 0:C * E]).then_inc(f_free[0], 1)
            act.wait_ge(f_free[0], NW // 2 + 1)
            act.sem_inc(wT_done[0], 1)

            def batch(b):
                used = [0, 0]

                def f_wait(i):
                    used[i] += 1
                    if counts(f_use(i, b, used[i])):
                        act.wait_ge(f_full[i], f_use(i, b, used[i]))
                    return FB[i]

                F = f_wait(0)
                Fc = F[:, 0:C * KV].rearrange("p (c k) -> p c k", c=C)
                for j in range(4):
                    act.copy(ctxT_rem[:, :, j, 0:REM], Fc[:, :, P:KV])
                act.copy(ctxT[:, :, 0:KV], Fc).then_inc(ctxT_done, 1)
                act.wait_ge(ctxT_done, b + 1)
                act.sem_inc(f_free[0], 1)
                F = f_wait(1)
                if counts(b * 16 * 12):
                    act.wait_ge(kstack_in, b * 16 * 12)
                if counts(b):
                    act.wait_ge(kblock_done, b)
                act.copy(kp[0][:, :, :].rearrange("p c k -> p (c k)"), F[:, 0:C * KVP]).then_inc(k1_done, 1)
                F = f_wait(0)
                if counts(b):
                    act.wait_ge(kv_cur, b)
                for par in range(2):
                    act.copy(v_next[:, :, par, :, 16 * par:16 * par + 16],
                             F[:, 0:D].rearrange("p (r s j d) -> p r s j d", r=2, s=2, j=4)[:, :, par])
                for par in range(2):
                    for j in range(4):
                        ins = act.copy(vr_next[32 * j:32 * j + 32, :, par, j, 16 * par:16 * par + 16],
                                       F[32 * j:32 * j + 32, D:2 * D].rearrange("p (r s j d) -> p r s j d", r=2, s=2, j=4)[:, :, par, j])
                ins.then_inc(v_done, 1)
                act.wait_ge(v_done, b + 1)
                act.sem_inc(f_free[0], 1)
                for hf in range(NH):
                    for c in range(C):
                        F = f_wait((c + 1) % 2)
                        act.copy(xnT[:, c, hf * HALF:(hf + 1) * HALF], F[:, :]).then_inc(xnT_done, 1)
                        act.wait_ge(xnT_done, b * 4 + hf * 2 + c + 1)
                        act.sem_inc(f_free[(c + 1) % 2], 1)
                for hf in range(NH):
                    for c in range(C):
                        k = hf * 2 + c
                        F = f_wait((c + 1) % 2)
                        if counts(b * 16 * len(PARTS)):
                            act.wait_ge(qstack_in[c][hf], b * 16 * len(PARTS))
                        act.copy(qp[0][:, c, hf * HALF:(hf + 1) * HALF], F[:, :]).then_inc(q1_done, 1)
                        act.wait_ge(rq_done, b * 4 + k + 1)
                        act.copy(qp[1][:, c, hf * HALF:(hf + 1) * HALF], rq[:, k % 2, :]).then_inc(q2_done, 1)
                for hf in range(NH):
                    F = f_wait(1 - hf)
                    if counts(b * 16):
                        act.wait_ge(m_in[hf], b * 16)
                    act.mul(nmT[:, hf * HALF:(hf + 1) * HALF], F[0:H, :], -1.0).then_inc(nmT_done, 1)
                    act.wait_ge(nmT_done, b * NH + hf + 1)
                    act.sem_inc(f_free[1 - hf], 1)

                def pv_copy(u):
                    act.wait_ge(o_full[u % 2], b * UO + u // 2 + 1)
                    if u >= 2:
                        if counts(b * NU + u - 1):
                            act.wait_ge(pvn_done, b * NU + u - 1)
                        if counts(b * NU * 16 + 16 * (u - 1)):
                            act.wait_ge(den_in, b * NU * 16 + 16 * (u - 1))
                    else:
                        if counts(b * NU):
                            act.wait_ge(pvn_done, b * NU)
                    act.copy(pv[:, u % 2, :], OB[u % 2][:, :]).then_inc(pv_out, 1)
                    act.wait_ge(pv_out, b * NU + u + 1)
                    act.sem_inc(o_free[u % 2], 1)

                for u in range(NU):
                    if u >= 2:
                        if counts(b * UO + u // 2):
                            act.wait_ge(o_full[u % 2], b * UO + u // 2)
                    else:
                        if counts(b * UO):
                            act.wait_ge(o_full[u % 2], b * UO)
                    for k in range(5):
                        m = 5 * u + k
                        act.wait_ge(s_full[m % 2], b * US + m // 2 + 1)
                        act.activation(probs[:, u % 2, k, :], SB_[m % 2][:, :], ACT.Exp, scale=SCALE).then_inc(probs_done, 1)
                    if u >= 1:
                        pv_copy(u - 1)
                pv_copy(NU - 1)
                used[0] += 4
                used[1] += 4
                for tp in range(T // 2):
                    i = (tp + 1) % 2
                    F = f_wait(i)
                    act.copy(xn2T[:, :, 2 * tp * P:(2 * tp + 2) * P], F[:, :].rearrange("p (c k) -> p c k", c=C)).then_inc(xn2T_done, 1)
                    act.wait_ge(xn2T_done, b * 4 + tp + 1)
                    act.sem_inc(f_free[i], 1)
                act.wait_ge(lg_done, b + 1)
                act.activation(ex[:, :, :], ex[:, :, :], ACT.Exp).then_inc(ex_done, 1)

            batch(0)
            with act.Fori(1, B) as b:
                batch(b)

        @block.vector
        def _(dve):
            dve.wait_ge(weights_in, 64)
            for par in range(2):
                ins = dve.tensor_copy(wop[:, :, :].rearrange("p c (r j s d) -> p (c r) j s d", r=2, s=2, j=4)[:, :, :, par],
                                      wsb[:, 3].rearrange("p c (r s j d) -> p (c r) s j d", r=2, s=2, j=4)[:, :, par])
                ins.then_inc(wop_half, 1)
            dve.wait_ge(wop_half, 2)
            dve.sem_inc(wop_done, 1)
            dve.wait_ge(tanh_done, 1)
            for i in range(1, NW, 2):
                dve.wait_ge(f_full[1], i // 2 + 1)
                if i == 3:
                    dve.tensor_scalar(wT[:, i].rearrange("p c d -> p (c d)"), FB[1][:, :], tg[:, 0:1], None,
                                      ALU.mult).then_inc(f_free[1], 1)
                else:
                    dst = wT[:, i] if i < 4 else ewT[:, i - 4]
                    dve.tensor_copy(dst.rearrange("p c d -> p (c d)"), FB[1][:, :]).then_inc(f_free[1], 1)
                dve.wait_ge(f_free[1], i // 2 + 1)
                dve.sem_inc(wT_done[1], 1)
            dve.wait_ge(pool_consts, 1)
            dve.tensor_reduce(headmask[:, :], ident[:, :].rearrange("p (d h) -> p h d", h=HPC), AX_X,
                              ALU.max).then_inc(headmask_done, 1)
            dve.wait_ge(headmask_done, 1)

            def batch(b):
                used = [0, 0]
                counter = [0]

                def L(ins):
                    link(dve, dve_chain, counter, b * K_DVE, ins)

                def f_wait(i):
                    used[i] += 1
                    if counts(f_use(i, b, used[i])):
                        dve.wait_ge(f_full[i], f_use(i, b, used[i]))
                    return FB[i]

                def norm(which, src, dst, tiles, var_sem, pool_sem, ready, count, done):
                    for t in tiles:
                        if ready is not None:
                            ready(t)
                        L(dve.bn_stats(st6[:, which, t, :], src[:, t, :]))
                    dve.sem_inc(stats_seen, 1)
                    for t in tiles:
                        L(dve.bn_aggr(mv[:, which, t, :], st6[:, which, t, :])) if t == tiles[-1] else dve.bn_aggr(mv[:, which, t, :], st6[:, which, t, :])
                    sl = slice(tiles[0], tiles[-1] + 1)
                    dve.tensor_scalar(ve[:, which, sl], mv[:, which, sl, 1], EPS, None, ALU.add).then_inc(var_sem, 1)
                    dve.wait_ge(pool_sem, count)
                    L(dve.tensor_tensor(nt[:, which, sl], rs0[:, which, sl], rs0[:, which, sl], ALU.mult))
                    L(dve.tensor_tensor(nt[:, which, sl], nt[:, which, sl], ve[:, which, sl], ALU.mult))
                    L(dve.tensor_scalar(nt[:, which, sl], nt[:, which, sl], -0.5, 1.5, ALU.mult, ALU.add))
                    L(dve.tensor_tensor(rstd[:, which, sl], nt[:, which, sl], rs0[:, which, sl], ALU.mult))
                    for t in tiles:
                        dve.tensor_scalar(dst[:, t, :], src[:, t, :], mv[:, which, t, 0:1], rstd[:, which, t:t + 1],
                                          ALU.subtract, ALU.mult).then_inc(done, 1)

                F = f_wait(1)
                dve.wait_ge(k1_done, b + 1)
                L(dve.tensor_tensor(rk[:, :, :].rearrange("p c k -> p (c k)"), F[:, 0:C * KVP],
                                    kp[0][:, :, :].rearrange("p c k -> p (c k)"), ALU.subtract))
                dve.sem_inc(f_free[1], 1)
                L(dve.tensor_copy(kp[1][:, :, :], rk[:, :, :]))
                dve.tensor_tensor(kp[2][:, :, :], rk[:, :, :], kp[1][:, :, :], ALU.subtract).then_inc(k_parts, 2)
                for c in range(C):
                    L(dve.tensor_tensor(kblock[:, c], kp[0][:, c:c + 1, 0:KV].broadcast_to([P, HPC, KV]),
                                        headmask[:, :].unsqueeze(2).broadcast_to([P, HPC, KV]), ALU.mult))
                dve.sem_inc(kblock_done, 1)
                dve.wait_ge(x_in, 16 * (b + 1))
                norm(0, xt, xn, list(range(T)), var_done, rs0_done, None, b + 1, xn_done)
                for k in range(4):
                    hf, c = k // 2, k % 2
                    F = f_wait((c + 1) % 2)
                    dve.wait_ge(q1_done, b * 4 + k + 1)
                    if k >= 2:
                        if counts(b * 4 + k - 1):
                            dve.wait_ge(q3_done, b * 4 + k - 1)
                        if counts(b * 4 + k - 1):
                            dve.wait_ge(q2_done, b * 4 + k - 1)
                    else:
                        if counts(b * 4):
                            dve.wait_ge(q3_done, b * 4)
                    L(dve.tensor_tensor(rq[:, k % 2, :], F[:, :], qp[0][:, c, hf * HALF:(hf + 1) * HALF], ALU.subtract))
                    dve.sem_inc(f_free[(c + 1) % 2], 1)
                    dve.sem_inc(rq_done, 1)
                n = 0
                for t in range(T):
                    for c in range(C):
                        for lo, hi in HEADS3:
                            i = n % 2
                            dve.wait_ge(a_full[i], b * UA[i] + n // 2 + 1)
                            ins = dve.tensor_reduce(mx[:, t, c * HPC + lo:c * HPC + hi],
                                                    AB[i][:, 0:(hi - lo) * KV].rearrange("p (h k) -> p h k", k=KV),
                                                    AX_X, ALU.max)
                            ins.then_inc(a_free[i], 1)
                            n += 1
                    if t % TH == TH - 1:
                        if counts(b * UA[0] + n // 2):
                            dve.wait_ge(a_free[0], b * UA[0] + n // 2)
                        if counts(b * UA[1] + n // 2):
                            dve.wait_ge(a_free[1], b * UA[1] + n // 2)
                        dve.sem_inc(mx_done, 1)
                dve.wait_ge(kstack_in, (b + 1) * 16 * 12)
                dve.wait_ge(v_done, b + 1)
                for i in range(2):
                    if counts(b * US):
                        dve.wait_ge(s_full[i], b * US)
                    if counts(b * UO):
                        dve.wait_ge(o_full[i], b * UO)
                L(dve.tensor_copy(kstack[:, :, :], kstack_next[:, :, :]))
                L(dve.tensor_copy(v_cur[:, :, :, :, :].rearrange("p a b c d -> p (a b c d)"), v_next[:, :, :, :, :].rearrange("p a b c d -> p (a b c d)")))
                L(dve.tensor_copy(vr_cur[:, :, :, :, :].rearrange("p a b c d -> p (a b c d)"), vr_next[:, :, :, :, :].rearrange("p a b c d -> p (a b c d)")))
                dve.sem_inc(kv_cur, 1)
                for u, (hf, pr, par) in enumerate(UNITS):
                    dve.wait_ge(den_in, 16 * (b * NU + u + 1))
                    if u >= 2:
                        if counts(16 * (b * NU + u - 1)):
                            dve.wait_ge(rec_in, 16 * (b * NU + u - 1))
                    else:
                        if counts(16 * (b * NU)):
                            dve.wait_ge(rec_in, 16 * (b * NU))
                    dve.reciprocal(rec_pack[:, u % 2, :], den_pack[:, u % 2, :]).then_inc(rec_done, 1)
                    dve.wait_ge(rec_in, 16 * (b * NU + u + 1))
                    dve.sem_inc(rec_seen, 1)
                    row, zero = 16 * (1 - par), 8
                    mask = ([row] * 16 + [zero] * 16) if par == 0 else ([zero] * 16 + [row] * 16)
                    L(dve.stream_shuffle(rec_b[:, u % 2, :], rec_row[:, u % 2, :], mask))
                    if u >= 2:
                        if counts(b * 4 + u // 2):
                            dve.wait_ge(attn_done, b * 4 + u // 2)
                    else:
                        if counts(b * 4):
                            dve.wait_ge(attn_done, b * 4)
                    dve.tensor_tensor(pvn[:, u % 2, :], pv[:, u % 2, :], rec_b[:, u % 2, :], ALU.mult).then_inc(pvn_done, 1)
                dve.wait_ge(xr_in, 16 * (b + 1))
                if counts(b * T):
                    dve.wait_ge(out_done, b * T)

                used[0] += 1 + 0
                used[1] += 1

                used[0] += 4
                used[1] += 2
                for t in range(T):
                    i = (t + 1) % 2
                    F = f_wait(i)
                    L(dve.tensor_tensor(x1[:, t, :], F[:, 0:D], xr[:, t, :], ALU.add))
                    dve.sem_inc(f_free[i], 1)
                    dve.sem_inc(x1_done, 1)
                norm(1, x1, xn2, list(range(T)), var2_done, rs02_done, None, b + 1, xn2_done)
                used[0] += 2
                used[1] += 2
                F = f_wait(1)
                L(dve.tensor_tensor(lg[:, :, :], F[:, 0:T * E].rearrange("p (t e) -> p t e", e=E),
                                    rb[:, :].unsqueeze(1).broadcast_to([P, T, E]), ALU.add))
                dve.sem_inc(f_free[1], 1)
                L(dve.tensor_reduce(lm[:, :], lg[:, :, :], AX_X, ALU.max))
                lmb = lm[:, :].unsqueeze(2).broadcast_to([P, T, E])
                L(dve.tensor_tensor(ex[:, :, :], lg[:, :, :], lmb, ALU.subtract))
                dve.sem_inc(lg_done, 1)
                L(dve.tensor_tensor(eq[:, :, :], lg[:, :, :], lmb, ALU.is_equal))
                L(dve.tensor_tensor(eq[:, :, :], eq[:, :, :], rev[:, :].unsqueeze(1).broadcast_to([P, T, E]), ALU.mult))
                L(dve.tensor_reduce(lm[:, :], eq[:, :, :], AX_X, ALU.max))
                L(dve.tensor_tensor(oh[:, :, :], eq[:, :, :], lmb, ALU.is_equal))
                dve.wait_ge(ex_done, b + 1)
                L(dve.tensor_reduce(wt[:, :], ex[:, :, :], AX_X, ALU.add))
                L(dve.reciprocal(wt[:, :], wt[:, :]))
                L(dve.tensor_scalar(wt[:, :], wt[:, :], tg[:, 1:2], None, ALU.mult))
                if counts(16 * b):
                    dve.wait_ge(out_written, 16 * b)
                for t in range(T):
                    for e2 in range(E // 2):
                        i = n % 2
                        dve.wait_ge(a_full[i], b * UA[i] + n // 2 + 1)
                        for s in range(2):
                            e = 2 * e2 + s
                            if e == 0:
                                L(dve.tensor_scalar(ybuf[:, t % 2, :], AB[i][:, 0:D], oh[:, t, e:e + 1], None, ALU.mult))
                            else:
                                L(dve.scalar_tensor_tensor(ybuf[:, t % 2, :], AB[i][:, s * D:(s + 1) * D], oh[:, t, e:e + 1],
                                                           ybuf[:, t % 2, :], ALU.mult, ALU.add))
                        dve.sem_inc(a_free[i], 1)
                        n += 1
                    dve.scalar_tensor_tensor(ob[:, t, :], ybuf[:, t % 2, :], wt[:, t:t + 1], x1[:, t, :],
                                             ALU.mult, ALU.add).then_inc(out_done, 1)
                assert used == UF, used
                assert counter[0] == K_DVE

            batch(0)
            with dve.Fori(1, B) as b:
                batch(b)

        @block.gpsimd
        def _(pool):
            counter = [0]

            def L0(ins):
                link(pool, pool_chain, counter, 0, ins)

            L0(pool.memset(ident[:, :], 0.0))
            L0(pool.affine_select(out=ident[:, :], in_=ident[:, :], compare_op=ALU.not_equal, fill=1.0, base=0,
                                  pattern=[[-1, P]], channel_multiplier=1))
            for e in range(E):
                L0(pool.memset(rev[:, e:e + 1], float(E - e)))
            L0(pool.memset(neg_half[:, :], -0.5))
            L0(pool.memset(ones_row[:, :], 1.0))
            L0(pool.memset(rec_row[:, :, :], 0.0))
            L0(pool.memset(ctxT[:, :, :], 0.0))
            L0(pool.memset(ctxT_rem[:, :, :, :], 0.0))
            L0(pool.memset(kstack_next[:, :, P:KVP], 0.0))
            L0(pool.memset(kstack_next[MROW:MROW + 1, :, 0:KV], 1.0))
            L0(pool.memset(v_next[:, :, :, :, :], 0.0))
            L0(pool.memset(vr_next[:, :, :, :, :], 0.0))
            for par in range(2):
                col = 16 * (1 - par)
                L0(pool.memset(v_next[:, :, par, :, col:col + 1], 1.0))
                for j in range(4):
                    L0(pool.memset(vr_next[32 * j:32 * j + REM, :, par, j, col:col + 1], 1.0))
            pool.sem_inc(pool_consts, 1)
            base = counter[0]

            def batch(b):
                counter = [0]

                def L(ins):
                    counter[0] += 1
                    ins.then_inc(pool_chain, 1)
                    if counts(base + b * K_POOL + counter[0]):
                        pool.wait_ge(pool_chain, base + b * K_POOL + counter[0])

                pool.wait_ge(var_done, b + 1)
                pool.tensor_tensor(rs0[:, 0, :], ve[:, 0, :], neg_half[:, :], ALU.pow).then_inc(rs0_done, 1)
                for k in range(4):
                    hf, c = k // 2, k % 2
                    pool.wait_ge(q2_done, b * 4 + k + 1)
                    pool.tensor_tensor(qp[2][:, c, hf * HALF:(hf + 1) * HALF], rq[:, k % 2, :],
                                       qp[1][:, c, hf * HALF:(hf + 1) * HALF], ALU.subtract).then_inc(q3_done, 1)
                for k in range(4):
                    hf, pr = k // 2, k % 2
                    pool.wait_ge(pvn_done, b * NU + 2 * k + 2)
                    if counts(b * T):
                        pool.wait_ge(x1_done, b * T)
                    pool.tensor_tensor(attnT[:, pr, hf * HALF:(hf + 1) * HALF], pvn[:, 0, :], pvn[:, 1, :],
                                       ALU.add).then_inc(attn_done, 1)
                pool.wait_ge(var2_done, b + 1)
                pool.tensor_tensor(rs0[:, 1, :], ve[:, 1, :], neg_half[:, :], ALU.pow).then_inc(rs02_done, 1)

            batch(0)
            with pool.Fori(1, B) as b:
                batch(b)

_INS = ["x", "ctx_1024", "g_xattn", "g_ffn", "L0_xattn_w_q", "L0_xattn_w_k", "L0_xattn_w_v", "L0_xattn_w_o",
        "L0_ffn_router_w", "L0_ffn_router_b", "L0_ffn_expert_w", "L0_ffn_expert_b"]


def kernel(**inputs):
    import numpy as _np
    import concourse.bacc as _bacc
    from concourse import mybir as _mybir
    from concourse.bass_utils import run_bass_kernel_spmd as _run

    nc = _bacc.Bacc("TRN2", target_bir_lowering=False, num_devices=1)
    arrays, args = {}, []
    for name in _INS:
        a = _np.ascontiguousarray(inputs[name])
        arrays[f"in_{name}"] = a
        args.append(nc.dram_tensor(f"in_{name}", a.shape, _mybir.dt.from_np(a.dtype), kind="ExternalInput").ap())
    args.append(nc.dram_tensor("out_0", inputs["x"].shape, _mybir.dt.float32, kind="ExternalOutput").ap())
    gated_block(nc, *args)
    r = _run(nc, [arrays], core_ids=[0])
    return r.results[0]["out_0"]
```

```python
from contextlib import ExitStack

import concourse.bass as bass
from concourse import mybir

P = 128
ALU = mybir.AluOpType
ACT = mybir.ActivationFunctionType
F32 = mybir.dt.float32
BF16 = mybir.dt.bfloat16
I32 = mybir.dt.int32
AX_X = mybir.AxisListType.X
EPS = 1e-5

STEPS = 40
FRONT = {
    "norm1_stats": {-7: 0, -5: 1}, "norm1_power": {-6: 0, -4: 1}, "norm1_apply": {-3: 0, -1: 1},
    "ctx_turn": {0: 0}, "ctx_copy": {1: 0}, "keys": {1: 0}, "key_parts": {2: 0}, "values": {2: 0}, "value_copy": {3: 0},
    "kstack_load": {4: 0},
    "x_turn": {3: 0, 4: 1, 5: 2, 6: 3}, "x_turn_copy": {4: 0, 5: 1, 6: 2, 7: 3},
    "query": {8: 0, 9: 1, 22: 2, 23: 3}, "query_part1": {9: 0, 10: 1, 23: 2, 24: 3}, "query_rest": {9: 0, 10: 1, 23: 2, 24: 3},
    "query_part2": {10: 0, 11: 1, 24: 2, 25: 3}, "query_part3": {10: 0, 11: 1, 24: 2, 25: 3},
    "rough": {(10 if n < 24 else 13) + n // 2: n // 2 for n in range(48)},
    "max_turn": {24: 0, 38: 1}, "max_copy": {25: 0, 39: 1},
    "qstack_load": {21: 0, 41: 1}, "max_load": {26: 0, 42: 1},
    "x_load": {-10: 0}, "ctx_load": {-30: 0},
}
UNIT = {
    "weigh": 6, "weigh_copy": 7, "den_load": 7, "den_recip": 9, "rec_load": 9, "normalise": 11, "join": 12,
}
BACK = {
    "residual_load": {-20: 0},
    "project": {-9: 0, -8: 1, -7: 2, -6: 3, 9: 4, 10: 5, 11: 6, 12: 7},
    "residual": {-8: 0, -7: 1, -6: 2, -5: 3, 10: 4, 11: 5, 12: 6, 13: 7},
    "norm2_stats": {-4: 0, 14: 1}, "norm2_power": {-3: 0, 15: 1}, "norm2_apply": {-2: 0, 16: 1},
    "x2_turn": {0: 0, 1: 1, 18: 2, 19: 3}, "x2_turn_copy": {1: 0, 2: 1, 19: 2, 20: 3},
    "logits": {3: 0, 21: 1}, "route": {4: 0, 22: 1}, "route_exp": {5: 0, 23: 1}, "route_weight": {6: 0, 24: 1},
    "rank": {23: 0}, "place": {24: 0}, "scatter": {25: 0}, "sorted_load": {31: 0, 32: 1, 43: 2},
    "sorted_turn": {34 + s: s for s in range(15)}, "sorted_turn_copy": {35 + s: s for s in range(15)},
    "expert": {36 + s: s for s in range(15)}, "expert_bias": {37 + s: s for s in range(15)},
    "sorted_store": {42: 0, 47: 1, 52: 2}, "gather": {54: 0}, "combine": {58: 0}, "out_store": {59: 0},
}


def steps_of(table, name, start):
    return {start + at: i for at, i in table[name].items()}


def gated_block(nc, x, ctx, g_xattn, g_ffn, w_q, w_k, w_v, w_o, router_w, router_b, expert_w, expert_b, out,
                sorted_rows, expert_rows):
    B, S, D = x.shape
    KV = ctx.shape[1]
    E = router_w.shape[0]
    H = 16
    HD = D // H
    T = S // P
    C = D // P
    HPC = P // HD
    REM = KV - P
    KVP = P + 32
    HALF = 512
    NH = S // HALF
    TH = HALF // P
    SCALE = float(HD) ** -0.5
    PARTS = [(0, 0), (0, 1), (0, 2), (1, 0), (1, 1), (2, 0)]
    NP = len(PARTS)
    MROW = NP * HD
    KROWS = MROW + 1
    UNITS = [(hf, pr, par) for hf in range(NH) for pr in range(2) for par in range(2)]
    NU = len(UNITS)
    HEADS3 = [(0, 3), (3, 6), (6, 8)]
    ST = T + E - 1
    SC = ST // 3
    FIRST, LAST = -STEPS - 8, STEPS * (B + 1) + 64

    def now(table, name, b, step):
        start = STEPS * (b - 1) if table is FRONT else STEPS * (b + 1)
        at = step - start
        if table is FRONT and name in ("x_load", "ctx_load") and b == 0:
            return None
        return table[name].get(at)

    front_use, back_use = {}, {}
    for e in range(E):
        back_use["weight", 0, e] = e
    for i in range(6):
        front_use["weight", 0, i] = i
    for step in range(FIRST, LAST):
        for b in range(B):
            for name in ("ctx_turn", "keys", "values", "x_turn", "query", "rough", "max_turn"):
                i = now(FRONT, name, b, step)
                if i is not None:
                    for k in range(2 if name in ("values", "rough") else 1):
                        front_use[name, b, 2 * i + k if name in ("values", "rough") else i] = len(front_use)
            for name in ("project", "x2_turn", "logits", "rank", "sorted_turn"):
                i = now(BACK, name, b, step)
                if i is not None:
                    back_use[name, b, i] = len(back_use)

    with ExitStack() as es:
        def sb(name, shape, dt=F32):
            return es.enter_context(nc.sbuf_tensor(name, shape, dt))

        def sem(name):
            return es.enter_context(nc.semaphore(name))

        shared_a = sb("shared_a", [P, 2 * 5 * HALF])
        shared_b = sb("shared_b", [P, 2 * T * D])
        ewsb = shared_a[:, 0:E * C * D].rearrange("p (e c d) -> p e c d", e=E, c=C)
        probs = shared_a[:, :].rearrange("p (a k n) -> p a k n", a=2, k=5)
        wsb = shared_b[:, 0:4 * C * D].rearrange("p (e c d) -> p e c d", e=4, c=C)
        wop = shared_b[:, 4 * C * D:5 * C * D].rearrange("p (c d) -> p c d", c=C)
        x1 = shared_b[:, :].rearrange("p (a t d) -> p a t d", a=2, t=T)

        ident = sb("ident", [P, P])
        before = sb("before", [P, P])
        ones = sb("ones", [P, P])
        headmask = sb("headmask", [P, HPC], BF16)
        wT = sb("wT", [P, 4, C, D])
        ewT = sb("ewT", [P, E, C, D])
        rwsb = sb("rwsb", [E, D])
        rwT = sb("rwT", [P, C, E])
        rb = sb("rb", [P, E])
        eb = sb("eb", [P, E, D])
        rev = sb("rev", [P, E])
        tile_no = sb("tile_no", [P, ST])
        tile_rows = sb("tile_rows", [P, T])
        gates = sb("gates", [P, 2])
        tg = sb("tg", [P, 2])
        neg_half = sb("neg_half", [P, T])

        ctxA = sb("ctxA", [P, D])
        ctxB = sb("ctxB", [REM, D])
        ctxT = sb("ctxT", [P, C, KVP])
        ctxT_rem = sb("ctxT_rem", [P, C, 4, 32])
        kp = [sb(f"kp{i}", [P, C, KVP], BF16) for i in range(3)]
        rk = sb("rk", [P, C, KVP])
        kblock = sb("kblock", [P, C, HPC, KV], BF16)
        kstack = sb("kstack", [KROWS, 2, H, KVP], BF16)
        vals = sb("vals", [P, 2, 2, 2, 4, 32])
        vrem = sb("vrem", [P, 2, 2, 2, 4, 32])

        xn = sb("xn", [P, T, D])
        xnT = sb("xnT", [P, C, S])
        st6 = sb("st6", [P, 2, T, 6])
        mv = sb("mv", [P, 2, T, 2])
        ve = sb("ve", [P, 2, T])
        rs0 = sb("rs0", [P, 2, T])
        nt = sb("nt", [P, 2, T])
        rstd = sb("rstd", [P, 2, T])
        qp = [sb("qp0", [P, C, S], BF16), sb("qp1", [P, C, HALF], BF16), sb("qp2", [P, C, HALF], BF16)]
        rq = sb("rq", [P, 2, HALF])
        qstack = sb("qstack", [KROWS, H, S], BF16)
        mx = sb("mx", [P, T, H])
        nmT = sb("nmT", [H, S], BF16)
        pv = sb("pv", [P, HALF])
        den_pack = sb("den_pack", [P, 2, HALF // 32])
        rec_pack = sb("rec_pack", [P, 2, HALF // 32])
        rec_row = sb("rec_row", [P, HALF])
        pvn = sb("pvn", [P, 2, HALF])
        attnT = sb("attnT", [P, 2, S])

        xn2 = sb("xn2", [P, T, D])
        x2T = sb("x2T", [P, C, HALF])
        lg = sb("lg", [P, T, E])
        lm = sb("lm", [P, T])
        eq = sb("eq", [P, T, E])
        oh = sb("oh", [P, T, E])
        ex = sb("ex", [P, T, E])
        wt = sb("wt", [P, 2, T])
        counts_e = sb("counts_e", [P, E])
        over = sb("over", [P, E, T])
        tiles_e = sb("tiles_e", [P, E])
        upto_e = sb("upto_e", [P, E])
        base_e = sb("base_e", [P, E])
        pos = sb("pos", [P, T, E])
        posf = sb("posf", [P, T])
        idx = sb("idx", [P, T], I32)
        past = sb("past", [P, ST, E])
        tile_ef = sb("tile_ef", [P, ST])
        tile_e = sb("tile_e", [P, ST], I32)
        xs = sb("xs", [P, 2 * SC, D])
        xsT = sb("xsT", [P, 2, D])
        yg = xn

        bank = [es.enter_context(nc.psum_tensor(f"bank{i}", [P, 512], F32)) for i in range(8)]
        front_bank, back_bank, score_bank, weigh_bank, expert_bank = bank[0:2], bank[2:4], bank[4:6], bank[6], bank[7]

        front_full = [sem(f"front_full{i}") for i in range(2)]
        front_free = [sem(f"front_free{i}") for i in range(2)]
        back_full = [sem(f"back_full{i}") for i in range(2)]
        back_free = [sem(f"back_free{i}") for i in range(2)]
        score_full = [sem(f"score_full{i}") for i in range(2)]
        weigh_full = sem("weigh_full")
        weigh_free = sem("weigh_free")
        expert_full = sem("expert_full")
        expert_free = sem("expert_free")
        weights_in = sem("weights_in")
        small_in = sem("small_in")
        experts_in = sem("experts_in")
        consts_done = sem("consts_done")
        headmask_done = sem("headmask_done")
        wop_half = sem("wop_half")
        tanh_done = sem("tanh_done")
        zeroed = sem("zeroed")
        ctx_in = sem("ctx_in")
        x_in = sem("x_in")
        residual_in = sem("residual_in")
        ctxT_done = sem("ctxT_done")
        k1_done = sem("k1_done")
        k_parts = sem("k_parts")
        kblock_done = sem("kblock_done")
        kstack_in = sem("kstack_in")
        v_done = sem("v_done")
        var1_done = sem("var1_done")
        pow1_done = sem("pow1_done")
        xn_done = sem("xn_done")
        xnT_done = sem("xnT_done")
        q1_done = sem("q1_done")
        rq_done = sem("rq_done")
        q2_done = sem("q2_done")
        q3_done = sem("q3_done")
        qstack_in = sem("qstack_in")
        nmT_done = sem("nmT_done")
        max_in = sem("max_in")
        probs_done = sem("probs_done")
        pv_out = sem("pv_out")
        den_in = sem("den_in")
        rec_done = sem("rec_done")
        rec_in = sem("rec_in")
        pvn_done = sem("pvn_done")
        attn_done = sem("attn_done")
        x1_done = sem("x1_done")
        var2_done = sem("var2_done")
        pow2_done = sem("pow2_done")
        xn2_done = sem("xn2_done")
        x2T_done = sem("x2T_done")
        shifted_done = sem("shifted_done")
        ex_done = sem("ex_done")
        oh_done = sem("oh_done")
        idx_done = sem("idx_done")
        scattered = sem("scattered")
        sorted_in = [sem(f"sorted_in{s}") for s in range(3)]
        xsT_done = sem("xsT_done")
        ys_done = sem("ys_done")
        ys_stored = [sem(f"ys_stored{s}") for s in range(3)]
        gathered = sem("gathered")
        out_done = sem("out_done")
        out_written = sem("out_written")
        dve_chain = sem("dve_chain")
        pool_chain = sem("pool_chain")

        block = es.enter_context(nc.Block())

        x_tiles = x.rearrange("b (p t) d -> b p t d", p=P)
        out_tiles = out.rearrange("b (p t) d -> b p t d", p=P)

        def slot(head):
            return head % HPC * C + head // HPC

        def part(i):
            return slice(i * HALF, (i + 1) * HALF)

        @block.sync
        def _(sp):
            sp.dma_start(xn[:, :, :], x_tiles[0]).then_inc(x_in, 16)
            sp.dma_start(ctxA[:, :], ctx[0, 0:P]).then_inc(ctx_in, 16)
            sp.dma_start(ctxB[:, :], ctx[0, P:KV]).then_inc(ctx_in, 16)
            for i, w in enumerate((w_k, w_v, w_q, w_o)):
                sp.dma_start(wsb[:, i], w.rearrange("(c p) d -> p c d", p=P)).then_inc(weights_in, 16)
            sp.dma_start(rwsb[:, :], router_w).then_inc(small_in, 16)
            sp.dma_start(rb[:, :], router_b.rearrange("(a e) -> a e", a=1).broadcast_to([P, E])).then_inc(small_in, 16)
            sp.dma_start(gates[:, 0:1], g_xattn.rearrange("(a e) -> a e", a=1).broadcast_to([P, 1])).then_inc(small_in, 16)
            sp.dma_start(gates[:, 1:2], g_ffn.rearrange("(a e) -> a e", a=1).broadcast_to([P, 1])).then_inc(small_in, 16)
            sp.dma_start(ewsb[:, :, :, :], expert_w.rearrange("e (c p) d -> p e c d", p=P)).then_inc(experts_in, 16)
            sp.dma_start(eb[:, :, :].rearrange("p e d -> p (e d)"),
                         expert_b.rearrange("(a e) d -> a (e d)", a=1).broadcast_to([P, E * D])).then_inc(small_in, 16)
            sp.wait_ge(consts_done, 1)
            for s in range(ST):
                sp.dma_start(sorted_rows[s * P:(s + 1) * P, :], rec_row[:, 0:D]).then_inc(zeroed, 16)

            for step in range(FIRST, LAST):
                for b in range(B):
                    if now(FRONT, "ctx_load", b, step) is not None:
                        sp.wait_ge(ctxT_done, b)
                        sp.dma_start(ctxA[:, :], ctx[b, 0:P]).then_inc(ctx_in, 16)
                        sp.dma_start(ctxB[:, :], ctx[b, P:KV]).then_inc(ctx_in, 16)
                    if now(FRONT, "x_load", b, step) is not None:
                        sp.wait_ge(xnT_done, 4 * b)
                        if b >= 4:
                            sp.wait_ge(out_written, 16 * (b - 3))
                        sp.dma_start(xn[:, :, :], x_tiles[b]).then_inc(x_in, 16)
                    if now(FRONT, "kstack_load", b, step) is not None:
                        sp.wait_ge(k1_done, b + 1)
                        sp.wait_ge(k_parts, b + 1)
                        if b >= 2:
                            sp.wait_ge(score_full[0], 20 * (b - 1))
                            sp.wait_ge(score_full[1], 20 * (b - 1))
                        for n, (_, k) in enumerate(PARTS):
                            sp.dma_start(kstack[n * HD:(n + 1) * HD, b % 2], kp[k][:, :, :]).then_inc(kstack_in, 16)
                    hf = now(FRONT, "qstack_load", b, step)
                    if hf is not None:
                        sp.wait_ge(q1_done, 4 * b + 2 * hf + 2)
                        sp.wait_ge(q2_done, 4 * b + 2 * hf + 2)
                        sp.wait_ge(q3_done, 4 * b + 2 * hf + 2)
                        if b >= 1:
                            sp.wait_ge(score_full[0], 20 * (b - 1) + 10 * hf + 10)
                            sp.wait_ge(score_full[1], 20 * (b - 1) + 10 * hf + 10)
                        for n, (q, _) in enumerate(PARTS):
                            sp.dma_start(qstack[n * HD:(n + 1) * HD, :, part(hf)],
                                         qp[q][:, :, part(hf if q == 0 else 0)]).then_inc(qstack_in, 16)
                    hf = now(FRONT, "max_load", b, step)
                    if hf is not None:
                        sp.wait_ge(nmT_done, NH * b + hf + 1)
                        if b >= 1:
                            sp.wait_ge(score_full[0], 20 * (b - 1) + 10 * hf + 10)
                            sp.wait_ge(score_full[1], 20 * (b - 1) + 10 * hf + 10)
                        sp.dma_start(qstack[MROW:MROW + 1, :, part(hf)], nmT[:, part(hf)]).then_inc(max_in, 16)
                for g in range(NU * B):
                    hf, pr, par = UNITS[g % NU]
                    row = 16 * (1 - par)
                    if step == 5 * g + UNIT["den_load"]:
                        sp.wait_ge(pv_out, g + 1)
                        if g >= 2:
                            sp.wait_ge(rec_done, g - 1)
                        sp.dma_start(den_pack[:, g % 2, :], pv[row:P:32, :]).then_inc(den_in, 16)
                    if step == 5 * g + UNIT["rec_load"]:
                        sp.wait_ge(rec_done, g + 1)
                        if g >= 1:
                            sp.wait_ge(pvn_done, g)
                        sp.dma_start(rec_row[row:P:32, :], rec_pack[:, g % 2, :]).then_inc(rec_in, 16)
                for b in range(B):
                    if now(BACK, "residual_load", b, step) is not None:
                        if b >= 2:
                            sp.wait_ge(out_done, T * (b - 1))
                        else:
                            sp.wait_ge(front_free[0], 2)
                            sp.wait_ge(front_free[1], 2)
                        sp.dma_start(x1[:, b % 2], x_tiles[b]).then_inc(residual_in, 16)
                    s = now(BACK, "sorted_load", b, step)
                    if s is not None:
                        sp.wait_ge(scattered, 16 * T * (b + 1))
                        if 3 * b + s >= 2:
                            sp.wait_ge(ys_stored[(s + 1) % 3], 16 * ((3 * b + s - 2) // 3 + 1))
                        sp.dma_start(xs[:, (3 * b + s) % 2 * SC:((3 * b + s) % 2 + 1) * SC, :],
                                     sorted_rows[s * SC * P:(s + 1) * SC * P, :].rearrange("(t p) d -> p t d", p=P)
                                     ).then_inc(sorted_in[s], 16)
                    s = now(BACK, "sorted_store", b, step)
                    if s is not None:
                        sp.wait_ge(ys_done, ST * b + SC * (s + 1))
                        if b >= 1:
                            sp.wait_ge(gathered, 16 * T * b)
                        sp.dma_start(expert_rows[s * SC * P:(s + 1) * SC * P, :].rearrange("(t p) d -> p t d", p=P),
                                     xs[:, (3 * b + s) % 2 * SC:((3 * b + s) % 2 + 1) * SC, :]).then_inc(ys_stored[s], 16)
                    if now(BACK, "out_store", b, step) is not None:
                        sp.wait_ge(out_done, T * (b + 1))
                        sp.dma_start(out_tiles[b], yg[:, :, :]).then_inc(out_written, 16)
            sp.wait_ge(out_written, 16 * B)

        @block.tensor
        def _(pe):
            def front_begin(name, b, i):
                n = front_use[name, b, i]
                if n >= 2:
                    pe.wait_ge(front_free[n % 2], n // 2)
                return front_bank[n % 2], front_full[n % 2]

            def back_begin(name, b, i):
                n = back_use[name, b, i]
                if n >= 2:
                    pe.wait_ge(back_free[n % 2], n // 2)
                return back_bank[n % 2], back_full[n % 2]

            def rough(b, n):
                t, c = n // 6, n // 3 % 2
                lo, hi = HEADS3[n % 3]
                pe.wait_ge(kblock_done, b + 1)
                pe.wait_ge(q1_done, 4 * b + 2 * (t // TH) + c + 1)
                F, full = front_begin("rough", b, n)
                pe.matmul(F[:, 0:(hi - lo) * KV], qp[0][:, c, t * P:(t + 1) * P], kblock[:, c, lo:hi, :],
                          start=True, stop=True).then_inc(full, 1)

            pe.wait_ge(consts_done, 1)
            for i in range(4):
                if i == 0:
                    pe.wait_ge(weights_in, 64)
                if i == 3:
                    pe.wait_ge(wop_half, 2)
                F, full = front_begin("weight", 0, i)
                for kc in range(C):
                    for oc in range(C):
                        src = wop[:, oc, kc * P:(kc + 1) * P] if i == 3 else wsb[:, i, oc, kc * P:(kc + 1) * P]
                        mm = pe.transpose(F[:, (kc * C + oc) * P:(kc * C + oc + 1) * P], src, ident[:, :])
                mm.then_inc(full, 1)
            pe.wait_ge(small_in, 80)
            for kc in range(C):
                F, full = front_begin("weight", 0, 4 + kc)
                pe.transpose(F[:, 0:E], rwsb[:, kc * P:(kc + 1) * P], ident[0:E, 0:E]).then_inc(full, 1)
            pe.wait_ge(front_free[0], 3)
            pe.wait_ge(front_free[1], 3)

            for step in range(FIRST, LAST):
                if 0 <= step < STEPS * B:
                    g, k = step // 5, step % 5
                    b, u = g // NU, g % NU
                    hf, pr, par = UNITS[u]
                    h0 = pr * 8 + par * 4
                    if k == 0:
                        if u == 0:
                            pe.wait_ge(kstack_in, 16 * NP * (b + 1))
                        if u % 4 == 0:
                            pe.wait_ge(qstack_in, 16 * NP * (NH * b + hf + 1))
                            pe.wait_ge(max_in, 16 * (NH * b + hf + 1))
                    if step >= 2:
                        pe.wait_ge(probs_done, step - 1)
                    sc = score_bank[step % 2]
                    if k < 4:
                        mm = pe.matmul(sc[:, :], kstack[:, b % 2, slot(h0 + k), 0:P], qstack[:, slot(h0 + k), part(hf)],
                                       start=True, stop=True)
                    else:
                        for j in range(4):
                            mm = pe.matmul(sc[32 * j:32 * j + 32, :], kstack[:, b % 2, slot(h0 + j), P:KVP],
                                           qstack[:, slot(h0 + j), part(hf)], start=True, stop=True)
                    mm.then_inc(score_full[step % 2], 1)

                for g in range(NU * B):
                    if step == 5 * g + UNIT["weigh"]:
                        b = g // NU
                        hf, pr, par = UNITS[g % NU]
                        o = weigh_bank
                        if g % NU == 0:
                            pe.wait_ge(v_done, b + 1)
                        if g >= 1:
                            pe.wait_ge(weigh_free, g)
                        pe.wait_ge(probs_done, 5 * g + 5)
                        for j in range(4):
                            pe.matmul(o[32 * j:32 * j + 32, :], vals[:, b % 2, pr, par, j, :], probs[:, g % 2, j, :],
                                      start=True, stop=False, skip_group_check=True)
                        pe.matmul(o[:, :], vrem[:, b % 2, pr, par, :, :], probs[:, g % 2, 4, :],
                                  start=False, stop=True, skip_group_check=True).then_inc(weigh_full, 1)

                for b in range(B):
                    if now(FRONT, "ctx_turn", b, step) is not None:
                        pe.wait_ge(ctx_in, 32 * (b + 1))
                        F, full = front_begin("ctx_turn", b, 0)
                        for kc in range(C):
                            pe.transpose(F[:, kc * KV:kc * KV + P], ctxA[:, kc * P:(kc + 1) * P], ident[:, :])
                            mm = pe.transpose(F[:, kc * KV + P:(kc + 1) * KV], ctxB[:, kc * P:(kc + 1) * P],
                                              ident[0:REM, 0:REM])
                        mm.then_inc(full, 1)
                    if now(FRONT, "keys", b, step) is not None:
                        pe.wait_ge(ctxT_done, b + 1)
                        F, full = front_begin("keys", b, 0)
                        for c in range(C):
                            for kc in range(C):
                                mm = pe.matmul(F[:, c * KVP:(c + 1) * KVP], wT[:, 0, kc, c * P:(c + 1) * P], ctxT[:, kc, :],
                                               start=kc == 0, stop=kc == C - 1)
                        mm.then_inc(full, 1)
                    if now(FRONT, "values", b, step) is not None:
                        F, full = front_begin("values", b, 0)
                        for kc in range(C):
                            mm = pe.matmul(F[:, 0:D], ctxT[:, kc, 0:P], wT[:, 1, kc, :], start=kc == 0, stop=kc == C - 1)
                        mm.then_inc(full, 1)
                        F, full = front_begin("values", b, 1)
                        for kc in range(C):
                            mm = pe.matmul(F[:, 0:D], ctxT_rem[:, kc].rearrange("p j k -> p (j k)"), wT[:, 1, kc, :],
                                           start=kc == 0, stop=kc == C - 1)
                        mm.then_inc(full, 1)
                    k = now(FRONT, "x_turn", b, step)
                    if k is not None:
                        hf, c = k // 2, k % 2
                        pe.wait_ge(xn_done, T * b + TH * (hf + 1))
                        F, full = front_begin("x_turn", b, k)
                        for t in range(TH):
                            mm = pe.transpose(F[:, t * P:(t + 1) * P], xn[:, hf * TH + t, c * P:(c + 1) * P], ident[:, :])
                        mm.then_inc(full, 1)
                    k = now(FRONT, "query", b, step)
                    if k is not None:
                        hf, c = k // 2, k % 2
                        pe.wait_ge(xnT_done, 4 * b + 2 * hf + 2)
                        F, full = front_begin("query", b, k)
                        for kc in range(C):
                            mm = pe.matmul(F[:, :], wT[:, 2, kc, c * P:(c + 1) * P], xnT[:, kc, part(hf)],
                                           start=kc == 0, stop=kc == C - 1)
                        mm.then_inc(full, 1)
                    k = now(FRONT, "rough", b, step)
                    if k is not None:
                        rough(b, 2 * k)
                    hf = now(FRONT, "max_turn", b, step)
                    if hf is not None:
                        for n in (front_use["rough", b, 24 * hf + 23], front_use["rough", b, 24 * hf + 22]):
                            pe.wait_ge(front_free[n % 2], n // 2 + 1)
                        F, full = front_begin("max_turn", b, hf)
                        for t in range(TH):
                            mm = pe.transpose(F[0:H, t * P:(t + 1) * P], mx[:, hf * TH + t, :], ident[:, :])
                        mm.then_inc(full, 1)

                if step == -2:
                    pe.wait_ge(experts_in, 16)
                    for e in range(E):
                        F, full = back_begin("weight", 0, e)
                        for kc in range(C):
                            for oc in range(C):
                                mm = pe.transpose(F[:, (kc * C + oc) * P:(kc * C + oc + 1) * P],
                                                  ewsb[:, e, oc, kc * P:(kc + 1) * P], ident[:, :])
                        mm.then_inc(full, 1)

                for b in range(B):
                    t = now(BACK, "project", b, step)
                    if t is not None:
                        pe.wait_ge(attn_done, 4 * b + 2 * (t // TH) + 2)
                        F, full = back_begin("project", b, t)
                        for pr in range(2):
                            mm = pe.matmul(F[:, 0:D], attnT[:, pr, t * P:(t + 1) * P], wT[:, 3, pr, :],
                                           start=pr == 0, stop=pr == 1)
                        mm.then_inc(full, 1)
                    k = now(BACK, "x2_turn", b, step)
                    if k is not None:
                        pe.wait_ge(xn2_done, T * b + 2 * k + 2)
                        F, full = back_begin("x2_turn", b, k)
                        for c in range(C):
                            for t in range(2):
                                mm = pe.transpose(F[:, (c * 2 + t) * P:(c * 2 + t + 1) * P],
                                                  xn2[:, 2 * k + t, c * P:(c + 1) * P], ident[:, :])
                        mm.then_inc(full, 1)
                    hf = now(BACK, "logits", b, step)
                    if hf is not None:
                        pe.wait_ge(x2T_done, 4 * b + 2 * hf + 2)
                        F, full = back_begin("logits", b, hf)
                        for t in range(TH):
                            for kc in range(C):
                                mm = pe.matmul(F[:, t * E:(t + 1) * E], x2T[:, kc, t * P:(t + 1) * P], rwT[:, kc, :],
                                               start=kc == 0, stop=kc == C - 1)
                        mm.then_inc(full, 1)
                    if now(BACK, "rank", b, step) is not None:
                        pe.wait_ge(oh_done, NH * (b + 1))
                        F, full = back_begin("rank", b, 0)
                        pe.matmul(F[:, 0:T * E], before[:, :], oh[:, :, :], start=True, stop=False, skip_group_check=True)
                        for s in range(1, T + 1):
                            mm = pe.matmul(F[:, s * E:(T + 1) * E], ones[:, :], oh[:, 0:T + 1 - s, :],
                                           start=False, stop=s == T, skip_group_check=True)
                        mm.then_inc(full, 1)
                    s = now(BACK, "sorted_turn", b, step)
                    if s is not None:
                        pe.wait_ge(sorted_in[s // SC], 16 * (b + 1))
                        F, full = back_begin("sorted_turn", b, s)
                        for c in range(C):
                            mm = pe.transpose(F[:, c * P:(c + 1) * P], xs[:, (3 * b + s // SC) % 2 * SC + s % SC, c * P:(c + 1) * P], ident[:, :])
                        mm.then_inc(full, 1)
                    s = now(BACK, "expert", b, step)
                    if s is not None:
                        pe.wait_ge(idx_done, b + 1)
                        e = pe.value_load(tile_e[0:1, s:s + 1], min_val=0, max_val=E - 1)
                        pe.wait_ge(xsT_done, ST * b + s + 1)
                        if ST * b + s >= 1:
                            pe.wait_ge(expert_free, ST * b + s)
                        for kc in range(C):
                            mm = pe.matmul(expert_bank[:, 0:D], xsT[:, s % 2, kc * P:(kc + 1) * P],
                                           ewT[:, bass.ds(e, 1), kc, :], start=kc == 0, stop=kc == C - 1)
                        mm.then_inc(expert_full, 1)
                for b in range(B):
                    k = now(FRONT, "rough", b, step)
                    if k is not None:
                        rough(b, 2 * k + 1)

        @block.scalar
        def _(act):
            def front_wait(name, b, i):
                n = front_use[name, b, i]
                act.wait_ge(front_full[n % 2], n // 2 + 1)
                return front_bank[n % 2], front_free[n % 2]

            def back_wait(name, b, i):
                n = back_use[name, b, i]
                act.wait_ge(back_full[n % 2], n // 2 + 1)
                return back_bank[n % 2], back_free[n % 2]

            act.wait_ge(small_in, 80)
            act.activation(tg[:, :], gates[:, :], ACT.Tanh).then_inc(tanh_done, 1)
            for i in (0, 2):
                F, free = front_wait("weight", 0, i)
                act.copy(wT[:, i].rearrange("p c (g d h) -> p (c g) d h", h=HPC, d=HD),
                         F[:, :].rearrange("p (g h d) -> p g d h", h=HPC, d=HD)).then_inc(free, 1)
            F, free = front_wait("weight", 0, 4)
            act.copy(rwT[:, 0, :], F[:, 0:E]).then_inc(free, 1)

            for step in range(FIRST, LAST):
                if 0 <= step < STEPS * B:
                    g, k = step // 5, step % 5
                    if g >= 2:
                        act.wait_ge(weigh_full, g - 1)
                    elif step == 0:
                        act.wait_ge(back_free[0], E // 2)
                        act.wait_ge(back_free[1], E // 2)
                    act.wait_ge(score_full[step % 2], step // 2 + 1)
                    act.activation(probs[:, g % 2, k, :], score_bank[step % 2][:, :], ACT.Exp, scale=SCALE
                                   ).then_inc(probs_done, 1)
                for g in range(NU * B):
                    if step == 5 * g + UNIT["weigh_copy"]:
                        act.wait_ge(weigh_full, g + 1)
                        if g >= 1:
                            act.wait_ge(pvn_done, g)
                            act.wait_ge(den_in, 16 * g)
                        act.copy(pv[:, :], weigh_bank[:, :]).then_inc(pv_out, 1)
                        act.wait_ge(pv_out, g + 1)
                        act.sem_inc(weigh_free, 1)
                for b in range(B):
                    if now(FRONT, "ctx_copy", b, step) is not None:
                        F, free = front_wait("ctx_turn", b, 0)
                        if b >= 1:
                            n = front_use["values", b - 1, 1]
                            act.wait_ge(front_full[n % 2], n // 2 + 1)
                        Fc = F[:, 0:C * KV].rearrange("p (c k) -> p c k", c=C)
                        for j in range(4):
                            act.copy(ctxT_rem[:, :, j, 0:REM], Fc[:, :, P:KV])
                        act.copy(ctxT[:, :, 0:KV], Fc).then_inc(ctxT_done, 1)
                        act.wait_ge(ctxT_done, b + 1)
                        act.sem_inc(free, 1)
                    if now(FRONT, "key_parts", b, step) is not None:
                        F, free = front_wait("keys", b, 0)
                        if b >= 1:
                            act.wait_ge(kstack_in, 16 * NP * b)
                            act.wait_ge(kblock_done, b)
                        act.copy(kp[0][:, :, :].rearrange("p c k -> p (c k)"), F[:, 0:C * KVP]).then_inc(k1_done, 1)
                    if now(FRONT, "value_copy", b, step) is not None:
                        if b >= 2:
                            act.wait_ge(weigh_full, NU * (b - 1))
                        F, free = front_wait("values", b, 0)
                        for par in range(2):
                            ins = act.copy(vals[:, b % 2, :, par, :, 16 * par:16 * par + 16],
                                           F[:, 0:D].rearrange("p (r s j d) -> p r s j d", r=2, s=2, j=4)[:, :, par])
                        ins.then_inc(free, 1)
                        F, free = front_wait("values", b, 1)
                        for par in range(2):
                            for j in range(4):
                                q = slice(32 * j, 32 * j + 32)
                                ins = act.copy(vrem[q, b % 2, :, par, j, 16 * par:16 * par + 16],
                                               F[q, 0:D].rearrange("p (r s j d) -> p r s j d", r=2, s=2, j=4)[:, :, par, j])
                        ins.then_inc(v_done, 1)
                        act.wait_ge(v_done, b + 1)
                        act.sem_inc(free, 1)
                    k = now(FRONT, "x_turn_copy", b, step)
                    if k is not None:
                        hf, c = k // 2, k % 2
                        if b >= 1 and k == 0:
                            n = front_use["query", b - 1, 3]
                            act.wait_ge(front_full[n % 2], n // 2 + 1)
                        F, free = front_wait("x_turn", b, k)
                        act.copy(xnT[:, c, part(hf)], F[:, :]).then_inc(xnT_done, 1)
                        act.wait_ge(xnT_done, 4 * b + k + 1)
                        act.sem_inc(free, 1)
                    k = now(FRONT, "query_part1", b, step)
                    if k is not None:
                        hf, c = k // 2, k % 2
                        F, free = front_wait("query", b, k)
                        if b >= 1:
                            act.wait_ge(qstack_in, 16 * NP * (NH * (b - 1) + hf + 1))
                            n = front_use["rough", b - 1, 24 * hf + 23]
                            act.wait_ge(front_full[n % 2], n // 2 + 1)
                        act.copy(qp[0][:, c, part(hf)], F[:, :]).then_inc(q1_done, 1)
                    k = now(FRONT, "query_part2", b, step)
                    if k is not None:
                        hf, c = k // 2, k % 2
                        act.wait_ge(rq_done, 4 * b + k + 1)
                        if NH * b + hf >= 1:
                            act.wait_ge(qstack_in, 16 * NP * (NH * b + hf))
                        act.copy(qp[1][:, c, :], rq[:, k % 2, :]).then_inc(q2_done, 1)
                    hf = now(FRONT, "max_copy", b, step)
                    if hf is not None:
                        F, free = front_wait("max_turn", b, hf)
                        if b >= 1:
                            act.wait_ge(max_in, 16 * (NH * (b - 1) + hf + 1))
                        act.mul(nmT[:, part(hf)], F[0:H, :], -1.0).then_inc(nmT_done, 1)
                        act.wait_ge(nmT_done, NH * b + hf + 1)
                        act.sem_inc(free, 1)
                if step == -2:
                    for e in range(0, E, 2):
                        F, free = back_wait("weight", 0, e)
                        act.copy(ewT[:, e].rearrange("p c d -> p (c d)"), F[:, :]).then_inc(free, 1)
                for b in range(B):
                    k = now(BACK, "x2_turn_copy", b, step)
                    if k is not None:
                        F, free = back_wait("x2_turn", b, k)
                        if k % 2 == 0 and 2 * b + k // 2 >= 1:
                            n = back_use["logits", b, 0] if k == 2 else back_use["logits", b - 1, 1]
                            act.wait_ge(back_full[n % 2], n // 2 + 1)
                        act.copy(x2T[:, :, (k % 2) * 2 * P:(k % 2 + 1) * 2 * P],
                                 F[:, :].rearrange("p (c k) -> p c k", c=C)).then_inc(x2T_done, 1)
                        act.wait_ge(x2T_done, 4 * b + k + 1)
                        act.sem_inc(free, 1)
                    hf = now(BACK, "route_exp", b, step)
                    if hf is not None:
                        act.wait_ge(shifted_done, NH * b + hf + 1)
                        ts = slice(hf * TH, (hf + 1) * TH)
                        act.activation(ex[:, ts, :], ex[:, ts, :], ACT.Exp).then_inc(ex_done, 1)
                    s = now(BACK, "sorted_turn_copy", b, step)
                    if s is not None:
                        F, free = back_wait("sorted_turn", b, s)
                        if ST * b + s >= 2:
                            act.wait_ge(expert_full, ST * b + s - 1)
                        act.copy(xsT[:, s % 2, :], F[:, 0:D]).then_inc(xsT_done, 1)
                        act.wait_ge(xsT_done, ST * b + s + 1)
                        act.sem_inc(free, 1)

        @block.vector
        def _(dve):
            done = [0]

            def link(ins):
                done[0] += 1
                ins.then_inc(dve_chain, 1)
                dve.wait_ge(dve_chain, done[0])

            def front_wait(name, b, i):
                n = front_use[name, b, i]
                dve.wait_ge(front_full[n % 2], n // 2 + 1)
                return front_bank[n % 2], front_free[n % 2]

            def back_wait(name, b, i):
                n = back_use[name, b, i]
                dve.wait_ge(back_full[n % 2], n // 2 + 1)
                return back_bank[n % 2], back_free[n % 2]

            def stats(which, src, hf, var_done):
                ts = range(hf * TH, (hf + 1) * TH)
                for t in ts:
                    ins = dve.bn_stats(st6[:, which, t, :], src[:, t, :])
                link(ins)
                for t in ts:
                    ins = dve.bn_aggr(mv[:, which, t, :], st6[:, which, t, :])
                link(ins)
                dve.tensor_scalar(ve[:, which, ts[0]:ts[-1] + 1], mv[:, which, ts[0]:ts[-1] + 1, 1], EPS, None,
                                  ALU.add).then_inc(var_done, 1)

            def normalise(which, src, dst, hf, rows_done):
                ts = slice(hf * TH, (hf + 1) * TH)
                link(dve.tensor_tensor(nt[:, which, ts], rs0[:, which, ts], rs0[:, which, ts], ALU.mult))
                link(dve.tensor_tensor(nt[:, which, ts], nt[:, which, ts], ve[:, which, ts], ALU.mult))
                link(dve.tensor_scalar(nt[:, which, ts], nt[:, which, ts], -0.5, 1.5, ALU.mult, ALU.add))
                link(dve.tensor_tensor(rstd[:, which, ts], nt[:, which, ts], rs0[:, which, ts], ALU.mult))
                for t in range(hf * TH, (hf + 1) * TH):
                    dve.tensor_scalar(dst[:, t, :], src[:, t, :], mv[:, which, t, 0:1], rstd[:, which, t:t + 1],
                                      ALU.subtract, ALU.mult).then_inc(rows_done, 1)

            dve.wait_ge(weights_in, 64)
            for par in range(2):
                dve.tensor_copy(wop[:, :, :].rearrange("p c (r j s d) -> p (c r) j s d", r=2, s=2, j=4)[:, :, :, par],
                                wsb[:, 3].rearrange("p c (r s j d) -> p (c r) s j d", r=2, s=2, j=4)[:, :, par]
                                ).then_inc(wop_half, 1)
            F, free = front_wait("weight", 0, 1)
            dve.tensor_copy(wT[:, 1].rearrange("p c d -> p (c d)"), F[:, :]).then_inc(free, 1)
            dve.wait_ge(tanh_done, 1)
            F, free = front_wait("weight", 0, 3)
            dve.tensor_scalar(wT[:, 3].rearrange("p c d -> p (c d)"), F[:, :], tg[:, 0:1], None, ALU.mult).then_inc(free, 1)
            F, free = front_wait("weight", 0, 5)
            dve.tensor_copy(rwT[:, 1, :], F[:, 0:E]).then_inc(free, 1)
            dve.wait_ge(consts_done, 1)
            dve.tensor_reduce(headmask[:, :], ident[:, :].rearrange("p (d h) -> p h d", h=HPC), AX_X,
                              ALU.max).then_inc(headmask_done, 1)
            dve.wait_ge(headmask_done, 1)

            def maxima(b, n):
                t, c = n // 6, n // 3 % 2
                lo, hi = HEADS3[n % 3]
                if b >= 1 and n % 24 == 0:
                    m = front_use["max_turn", b - 1, n // 24]
                    dve.wait_ge(front_full[m % 2], m // 2 + 1)
                F, free = front_wait("rough", b, n)
                dve.tensor_reduce(mx[:, t, :].rearrange("p (h c) -> p h c", c=C)[:, lo:hi, c],
                                  F[:, 0:(hi - lo) * KV].rearrange("p (h k) -> p h k", k=KV),
                                  AX_X, ALU.max).then_inc(free, 1)

            for step in range(FIRST, LAST):
                for b in range(B):
                    k = now(FRONT, "rough", b, step)
                    if k is not None:
                        maxima(b, 2 * k)
                    s = now(BACK, "expert_bias", b, step)
                    if s is not None:
                        dve.wait_ge(idx_done, b + 1)
                        e = dve.value_load(tile_e[0:1, s:s + 1], min_val=0, max_val=E - 1)
                        r = (3 * b + s // SC) % 2 * SC + s % SC
                        dve.wait_ge(expert_full, ST * b + s + 1)
                        dve.tensor_tensor(xs[:, r:r + 1, :], expert_bank[:, 0:D].unsqueeze(1), eb[:, bass.ds(e, 1), :],
                                          ALU.add).then_inc(ys_done, 1)
                        dve.wait_ge(ys_done, ST * b + s + 1)
                        dve.sem_inc(expert_free, 1)
                for b in range(B):
                    if now(FRONT, "key_parts", b, step) is not None:
                        F, free = front_wait("keys", b, 0)
                        dve.wait_ge(k1_done, b + 1)
                        link(dve.tensor_tensor(rk[:, :, :].rearrange("p c k -> p (c k)"), F[:, 0:C * KVP],
                                               kp[0][:, :, :].rearrange("p c k -> p (c k)"), ALU.subtract))
                        dve.sem_inc(free, 1)
                        link(dve.tensor_copy(kp[1][:, :, :], rk[:, :, :]))
                        dve.tensor_tensor(kp[2][:, :, :], rk[:, :, :], kp[1][:, :, :], ALU.subtract).then_inc(k_parts, 1)
                        if b >= 1:
                            n = front_use["rough", b - 1, 47]
                            dve.wait_ge(front_full[n % 2], n // 2 + 1)
                        for c in range(C):
                            ins = dve.tensor_tensor(kblock[:, c], kp[0][:, c:c + 1, 0:KV].broadcast_to([P, HPC, KV]),
                                                    headmask[:, :].unsqueeze(2).broadcast_to([P, HPC, KV]), ALU.mult)
                        ins.then_inc(kblock_done, 1)
                    hf = now(FRONT, "norm1_stats", b, step)
                    if hf is not None:
                        dve.wait_ge(x_in, 16 * (b + 1))
                        stats(0, xn, hf, var1_done)
                    hf = now(FRONT, "norm1_apply", b, step)
                    if hf is not None:
                        dve.wait_ge(pow1_done, NH * b + hf + 1)
                        normalise(0, xn, xn, hf, xn_done)
                    k = now(FRONT, "query_rest", b, step)
                    if k is not None:
                        hf, c = k // 2, k % 2
                        F, free = front_wait("query", b, k)
                        dve.wait_ge(q1_done, 4 * b + k + 1)
                        if 4 * b + k >= 2:
                            dve.wait_ge(q2_done, 4 * b + k - 1)
                            dve.wait_ge(q3_done, 4 * b + k - 1)
                        dve.tensor_tensor(rq[:, k % 2, :], F[:, :], qp[0][:, c, part(hf)], ALU.subtract
                                          ).then_inc(rq_done, 1)
                        dve.wait_ge(rq_done, 4 * b + k + 1)
                        dve.sem_inc(free, 1)
                if step == -2:
                    for e in range(1, E, 2):
                        F, free = back_wait("weight", 0, e)
                        dve.tensor_copy(ewT[:, e].rearrange("p c d -> p (c d)"), F[:, :]).then_inc(free, 1)
                for g in range(NU * B):
                    hf, pr, par = UNITS[g % NU]
                    if step == 5 * g + UNIT["den_recip"]:
                        dve.wait_ge(den_in, 16 * (g + 1))
                        if g >= 2:
                            dve.wait_ge(rec_in, 16 * (g - 1))
                        dve.reciprocal(rec_pack[:, g % 2, :], den_pack[:, g % 2, :]).then_inc(rec_done, 1)
                    if step == 5 * g + UNIT["normalise"]:
                        row, zero = 16 * (1 - par), 8
                        mask = ([row] * 16 + [zero] * 16) if par == 0 else ([zero] * 16 + [row] * 16)
                        dve.wait_ge(rec_in, 16 * (g + 1))
                        if g >= 2:
                            dve.wait_ge(attn_done, g // 2)
                        link(dve.stream_shuffle(pvn[:, g % 2, :], rec_row[:, :], mask))
                        dve.tensor_tensor(pvn[:, g % 2, :], pv[:, :], pvn[:, g % 2, :], ALU.mult).then_inc(pvn_done, 1)
                for b in range(B):
                    t = now(BACK, "residual", b, step)
                    if t is not None:
                        if t == 0:
                            dve.wait_ge(residual_in, 16 * (b + 1))
                        F, free = back_wait("project", b, t)
                        dve.tensor_tensor(x1[:, b % 2, t, :], F[:, 0:D], x1[:, b % 2, t, :], ALU.add).then_inc(x1_done, 1)
                        dve.wait_ge(x1_done, T * b + t + 1)
                        dve.sem_inc(free, 1)
                    hf = now(BACK, "norm2_stats", b, step)
                    if hf is not None:
                        stats(1, x1[:, b % 2], hf, var2_done)
                    hf = now(BACK, "norm2_apply", b, step)
                    if hf is not None:
                        dve.wait_ge(pow2_done, NH * b + hf + 1)
                        if b >= 1:
                            dve.wait_ge(scattered, 16 * T * b)
                        normalise(1, x1[:, b % 2], xn2, hf, xn2_done)
                    hf = now(BACK, "route", b, step)
                    if hf is not None:
                        ts = slice(hf * TH, (hf + 1) * TH)
                        full3 = [P, TH, E]
                        F, free = back_wait("logits", b, hf)
                        link(dve.tensor_tensor(lg[:, ts, :], F[:, 0:TH * E].rearrange("p (t e) -> p t e", e=E),
                                               rb[:, :].unsqueeze(1).broadcast_to(full3), ALU.add))
                        dve.sem_inc(free, 1)
                        link(dve.tensor_reduce(lm[:, ts], lg[:, ts, :], AX_X, ALU.max))
                        top = lm[:, ts].unsqueeze(2).broadcast_to(full3)
                        dve.tensor_tensor(ex[:, ts, :], lg[:, ts, :], top, ALU.subtract).then_inc(shifted_done, 1)
                        link(dve.tensor_tensor(eq[:, ts, :], lg[:, ts, :], top, ALU.is_equal))
                        link(dve.tensor_tensor(eq[:, ts, :], eq[:, ts, :], rev[:, :].unsqueeze(1).broadcast_to(full3), ALU.mult))
                        link(dve.tensor_reduce(lm[:, ts], eq[:, ts, :], AX_X, ALU.max))
                        dve.tensor_tensor(oh[:, ts, :], eq[:, ts, :], top, ALU.is_equal).then_inc(oh_done, 1)
                    hf = now(BACK, "route_weight", b, step)
                    if hf is not None:
                        ts = slice(hf * TH, (hf + 1) * TH)
                        w = wt[:, b % 2, ts]
                        dve.wait_ge(ex_done, NH * b + hf + 1)
                        link(dve.tensor_reduce(w, ex[:, ts, :], AX_X, ALU.add))
                        link(dve.reciprocal(w, w))
                        link(dve.tensor_scalar(w, w, tg[:, 1:2], None, ALU.mult))
                    if now(BACK, "place", b, step) is not None:
                        F, free = back_wait("rank", b, 0)
                        if b >= 1:
                            dve.wait_ge(gathered, 16 * T * b)
                            dve.wait_ge(expert_full, ST * b)
                        link(dve.tensor_copy(counts_e[:, :], F[:, T * E:(T + 1) * E]))
                        link(dve.tensor_tensor(over[:, :, :], counts_e[:, :].unsqueeze(2).broadcast_to([P, E, T]),
                                               tile_rows[:, :].unsqueeze(1).broadcast_to([P, E, T]), ALU.is_gt))
                        link(dve.tensor_reduce(tiles_e[:, :], over[:, :, :], AX_X, ALU.add))
                        link(dve.tensor_tensor_scan(upto_e[:, :], ones[:, 0:E], tiles_e[:, :], 0.0, ALU.mult, ALU.add))
                        link(dve.tensor_tensor(base_e[:, :], upto_e[:, :], tiles_e[:, :], ALU.subtract))
                        link(dve.tensor_scalar(base_e[:, :], base_e[:, :], float(P), None, ALU.mult))
                        link(dve.tensor_tensor(pos[:, :, :], F[:, 0:T * E].rearrange("p (t e) -> p t e", e=E),
                                               base_e[:, :].unsqueeze(1).broadcast_to([P, T, E]), ALU.add))
                        dve.sem_inc(free, 1)
                        link(dve.tensor_tensor(pos[:, :, :], pos[:, :, :], oh[:, :, :], ALU.mult))
                        link(dve.tensor_reduce(posf[:, :], pos[:, :, :], AX_X, ALU.add))
                        link(dve.tensor_copy(idx[:, :], posf[:, :]))
                        link(dve.tensor_tensor(past[:, :, :], upto_e[:, :].unsqueeze(1).broadcast_to([P, ST, E]),
                                               tile_no[:, :].unsqueeze(2).broadcast_to([P, ST, E]), ALU.is_le))
                        link(dve.tensor_reduce(tile_ef[:, :], past[:, :, :], AX_X, ALU.add))
                        link(dve.tensor_scalar(tile_ef[:, :], tile_ef[:, :], float(E - 1), None, ALU.min))
                        dve.tensor_copy(tile_e[:, :], tile_ef[:, :]).then_inc(idx_done, 1)
                    if now(BACK, "combine", b, step) is not None:
                        dve.wait_ge(gathered, 16 * T * (b + 1))
                        for t in range(T):
                            dve.scalar_tensor_tensor(yg[:, t, :], yg[:, t, :], wt[:, b % 2, t:t + 1], x1[:, b % 2, t, :],
                                                     ALU.mult, ALU.add).then_inc(out_done, 1)
                for b in range(B):
                    k = now(FRONT, "rough", b, step)
                    if k is not None:
                        maxima(b, 2 * k + 1)

        @block.gpsimd
        def _(pool):
            done = [0]

            def link(ins):
                done[0] += 1
                ins.then_inc(pool_chain, 1)
                pool.wait_ge(pool_chain, done[0])

            link(pool.memset(ident[:, :], 0.0))
            link(pool.affine_select(out=ident[:, :], in_=ident[:, :], compare_op=ALU.not_equal, fill=1.0, base=0,
                                    pattern=[[-1, P]], channel_multiplier=1))
            link(pool.memset(ones[:, :], 1.0))
            link(pool.affine_select(out=before[:, :], in_=ones[:, :], compare_op=ALU.is_gt, fill=0.0, base=0,
                                    pattern=[[1, P]], channel_multiplier=-1))
            for e in range(E):
                pool.memset(rev[:, e:e + 1], float(E - e))
            for s in range(ST):
                pool.memset(tile_no[:, s:s + 1], float(s))
            for t in range(T):
                pool.memset(tile_rows[:, t:t + 1], float(P * t))
            pool.memset(neg_half[:, :], -0.5)
            pool.memset(rec_row[:, :], 0.0)
            pool.memset(ctxT[:, :, :], 0.0)
            pool.memset(ctxT_rem[:, :, :, :], 0.0)
            link(pool.memset(kstack[:, :, :, P:KVP], 0.0))
            link(pool.memset(kstack[MROW:MROW + 1, :, :, 0:KV], 1.0))
            pool.memset(vals[:, :, :, :, :, :], 0.0)
            link(pool.memset(vrem[:, :, :, :, :, :], 0.0))
            for par in range(2):
                col = 16 * (1 - par)
                link(pool.memset(vals[:, :, :, par, :, col:col + 1], 1.0))
                for j in range(4):
                    link(pool.memset(vrem[32 * j:32 * j + REM, :, :, par, j, col:col + 1], 1.0))
            pool.sem_inc(consts_done, 1)

            for step in range(FIRST, LAST):
                for b in range(B):
                    hf = now(FRONT, "norm1_power", b, step)
                    if hf is not None:
                        ts = slice(hf * TH, (hf + 1) * TH)
                        pool.wait_ge(var1_done, NH * b + hf + 1)
                        pool.tensor_tensor(rs0[:, 0, ts], ve[:, 0, ts], neg_half[:, ts], ALU.pow).then_inc(pow1_done, 1)
                    k = now(FRONT, "query_part3", b, step)
                    if k is not None:
                        hf, c = k // 2, k % 2
                        pool.wait_ge(q2_done, 4 * b + k + 1)
                        if NH * b + hf >= 1:
                            pool.wait_ge(qstack_in, 16 * NP * (NH * b + hf))
                        pool.tensor_tensor(qp[2][:, c, :], rq[:, k % 2, :], qp[1][:, c, :],
                                           ALU.subtract).then_inc(q3_done, 1)
                for g in range(1, NU * B, 2):
                    if step == 5 * g + UNIT["join"]:
                        b = g // NU
                        hf, pr, par = UNITS[g % NU]
                        pool.wait_ge(pvn_done, g + 1)
                        if b >= 1:
                            pool.wait_ge(x1_done, T * (b - 1) + TH * (hf + 1))
                        pool.tensor_tensor(attnT[:, pr, part(hf)], pvn[:, 0, :], pvn[:, 1, :], ALU.add).then_inc(attn_done, 1)
                for b in range(B):
                    hf = now(BACK, "norm2_power", b, step)
                    if hf is not None:
                        ts = slice(hf * TH, (hf + 1) * TH)
                        pool.wait_ge(var2_done, NH * b + hf + 1)
                        pool.tensor_tensor(rs0[:, 1, ts], ve[:, 1, ts], neg_half[:, ts], ALU.pow).then_inc(pow2_done, 1)
                    if now(BACK, "scatter", b, step) is not None:
                        pool.wait_ge(idx_done, b + 1)
                        pool.wait_ge(xn2_done, T * (b + 1))
                        if b == 0:
                            pool.wait_ge(zeroed, 16 * ST)
                        else:
                            for s in range(3):
                                pool.wait_ge(sorted_in[s], 16 * b)
                        for t in range(T):
                            pool.indirect_dma_start(out=sorted_rows, out_offset=bass.IndirectOffsetOnAxis(ap=idx[:, t:t + 1], axis=0),
                                                    in_=xn2[:, t, :], in_offset=None).then_inc(scattered, 16)
                    if now(BACK, "gather", b, step) is not None:
                        for s in range(3):
                            pool.wait_ge(ys_stored[s], 16 * (b + 1))
                        pool.wait_ge(xnT_done, 4 * min(b + 4, B))
                        if b >= 1:
                            pool.wait_ge(out_written, 16 * b)
                        for t in range(T):
                            pool.indirect_dma_start(out=yg[:, t, :], out_offset=None, in_=expert_rows,
                                                    in_offset=bass.IndirectOffsetOnAxis(ap=idx[:, t:t + 1], axis=0)
                                                    ).then_inc(gathered, 16)


_INS = ["x", "ctx_1024", "g_xattn", "g_ffn", "L0_xattn_w_q", "L0_xattn_w_k", "L0_xattn_w_v", "L0_xattn_w_o",
        "L0_ffn_router_w", "L0_ffn_router_b", "L0_ffn_expert_w", "L0_ffn_expert_b"]


def kernel(**inputs):
    import numpy as _np
    import concourse.bacc as _bacc
    from concourse import mybir as _mybir
    from concourse.bass_utils import run_bass_kernel_spmd as _run

    nc = _bacc.Bacc("TRN2", target_bir_lowering=False, num_devices=1)
    arrays, args = {}, []
    for name in _INS:
        a = _np.ascontiguousarray(inputs[name])
        arrays[f"in_{name}"] = a
        args.append(nc.dram_tensor(f"in_{name}", a.shape, _mybir.dt.from_np(a.dtype), kind="ExternalInput").ap())
    _, s, d = inputs["x"].shape
    rows = s + (inputs["L0_ffn_router_w"].shape[0] - 1) * 128
    args.append(nc.dram_tensor("out_0", inputs["x"].shape, _mybir.dt.float32, kind="ExternalOutput").ap())
    args.append(nc.dram_tensor("sorted_rows", (rows, d), _mybir.dt.float32).ap())
    args.append(nc.dram_tensor("expert_rows", (rows, d), _mybir.dt.float32).ap())
    gated_block(nc, *args)
    r = _run(nc, [arrays], core_ids=[0])
    return r.results[0]["out_0"]
```

```python
from contextlib import ExitStack

import concourse.bass as bass
from concourse import mybir

P = 128
ALU = mybir.AluOpType
ACT = mybir.ActivationFunctionType
F32 = mybir.dt.float32
BF16 = mybir.dt.bfloat16
I32 = mybir.dt.int32
AX_X = mybir.AxisListType.X
EPS = 1e-5

STEPS = 40
FRONT = {
    "x_load": {-9: 0}, "ctx_load": {-23: 0}, "norm1_stats": {-6: 0, -4: 1}, "norm1_power": {-7: 0, -3: 1},
    "norm1_apply": {-4: 0, 0: 1}, "x_turn": {0: 0, 2: 1, 5: 2, 9: 3}, "x_turn_copy": {0: 0, 1: 1, 4: 2, 9: 3},
    "ctx_turn": {16: 0}, "ctx_copy": {15: 0}, "keys": {17: 0}, "key_parts": {17: 0}, "values": {19: 0},
    "value_copy": {19: 0}, "kstack_load": {21: 0}, "query": {21: 0, 22: 1, 38: 2, 39: 3},
    "query_part1": {21: 0, 22: 1, 38: 2, 40: 3}, "query_rest": {20: 0, 22: 1, 38: 2, 41: 3},
    "query_part2": {21: 0, 22: 1, 41: 2, 43: 3}, "query_part3": {21: 0, 25: 1, 44: 2, 45: 3},
    "rough": {47: 0, 48: 1, 49: 2, 50: 3, 51: 4, 52: 5, 53: 6, 54: 7, 55: 8, 56: 9, 57: 10, 58: 11, 59: 12, 60: 13,
        61: 14, 62: 15, 63: 16, 64: 17, 65: 18, 66: 19, 67: 20, 68: 21, 69: 22, 70: 23, 83: 24, 84: 25, 85: 26, 86: 27,
        87: 28, 88: 29, 91: 30, 92: 31, 93: 32, 94: 33, 95: 34, 96: 35, 100: 36, 101: 37, 102: 38, 103: 39, 104: 40,
        105: 41, 106: 42, 107: 43, 108: 44, 109: 45, 110: 46, 111: 47},
    "maxima": {46: 0, 47: 1, 48: 2, 49: 3, 50: 4, 51: 5, 52: 6, 53: 7, 54: 8, 55: 9, 56: 10, 57: 11, 60: 12, 61: 13,
        62: 14, 63: 15, 64: 16, 65: 17, 66: 18, 67: 19, 68: 20, 69: 21, 70: 22, 71: 23, 83: 24, 85: 25, 86: 26, 87: 27,
        88: 28, 90: 29, 92: 30, 93: 31, 94: 32, 95: 33, 96: 34, 97: 35, 100: 36, 101: 37, 102: 38, 103: 39, 104: 40,
        105: 41, 106: 42, 107: 43, 108: 44, 109: 45, 110: 46, 111: 47},
    "max_turn": {37: 0, 57: 1}, "max_copy": {36: 0, 57: 1}, "qstack_load": {26: 0, 45: 1}, "max_load": {36: 0, 56: 1},
}
FRONT_ALONE = {
    "x_load": {-10: 0}, "ctx_load": {-25: 0}, "norm1_stats": {-7: 0, -5: 1}, "norm1_power": {-6: 0, -4: 1},
    "norm1_apply": {-2: 0, 1: 1}, "x_turn": {-1: 0, 1: 1, 4: 2, 8: 3}, "x_turn_copy": {-3: 0, -1: 1, 4: 2, 9: 3},
    "ctx_turn": {16: 0}, "ctx_copy": {15: 0}, "keys": {19: 0}, "key_parts": {15: 0}, "values": {19: 0},
    "value_copy": {18: 0}, "kstack_load": {18: 0}, "query": {19: 0, 22: 1, 38: 2, 39: 3},
    "query_part1": {21: 0, 22: 1, 38: 2, 40: 3}, "query_rest": {20: 0, 22: 1, 38: 2, 41: 3},
    "query_part2": {21: 0, 23: 1, 42: 2, 44: 3}, "query_part3": {19: 0, 21: 1, 38: 2, 41: 3},
    "rough": {45: 0, 46: 1, 47: 2, 48: 3, 49: 4, 50: 5, 51: 6, 52: 7, 53: 8, 54: 9, 55: 10, 56: 11, 59: 12, 60: 13,
        61: 14, 62: 15, 63: 16, 64: 17, 65: 18, 66: 19, 67: 20, 68: 21, 69: 22, 70: 23, 83: 24, 84: 25, 85: 26, 86: 27,
        87: 28, 88: 29, 91: 30, 92: 31, 93: 32, 94: 33, 95: 34, 96: 35, 100: 36, 101: 37, 102: 38, 103: 39, 104: 40,
        105: 41, 106: 42, 107: 43, 108: 44, 109: 45, 110: 46, 111: 47},
    "maxima": {46: 0, 47: 1, 48: 2, 49: 3, 50: 4, 51: 5, 52: 6, 53: 7, 54: 8, 55: 9, 56: 10, 57: 11, 60: 12, 61: 13,
        62: 14, 63: 15, 64: 16, 65: 17, 66: 18, 67: 19, 68: 20, 69: 21, 70: 22, 71: 23, 83: 24, 85: 25, 86: 26, 87: 27,
        88: 28, 89: 29, 92: 30, 93: 31, 94: 32, 95: 33, 96: 34, 97: 35, 100: 36, 101: 37, 102: 38, 103: 39, 104: 40,
        105: 41, 106: 42, 107: 43, 108: 44, 109: 45, 110: 46, 111: 47},
    "max_turn": {37: 0, 57: 1}, "max_copy": {36: 0, 57: 1}, "qstack_load": {23: 0, 41: 1}, "max_load": {36: 0, 58: 1},
}
UNIT = {
    "weigh": 6, "weigh_copy": 6, "den_load": 6, "den_recip": 9, "rec_load": 9, "normalise": 11, "join": 13,
}
BACK = {
    "residual_load": {-18: 0}, "project": {-9: 0, -8: 1, -7: 2, -6: 3, 9: 4, 10: 5, 11: 6, 12: 7},
    "residual": {-8: 0, -7: 1, -6: 2, -5: 3, 10: 4, 11: 5, 12: 6, 15: 7}, "norm2_stats": {-5: 0, 15: 1},
    "norm2_power": {-6: 0, 12: 1}, "norm2_apply": {-2: 0, 16: 1}, "x2_turn": {0: 0, 1: 1, 18: 2, 20: 3},
    "x2_turn_copy": {-1: 0, 0: 1, 18: 2, 19: 3}, "logits": {3: 0, 23: 1}, "route": {4: 0, 22: 1},
    "route_exp": {10: 0, 33: 1}, "route_weight": {12: 0, 37: 1},
}
BACK_ALONE = {
    "residual_load": {-17: 0}, "project": {-9: 0, -8: 1, -7: 2, -6: 3, 9: 4, 10: 5, 11: 6, 12: 7},
    "residual": {-8: 0, -7: 1, -6: 2, -5: 3, 9: 4, 11: 5, 12: 6, 15: 7}, "norm2_stats": {-4: 0, 16: 1},
    "norm2_power": {-7: 0, 12: 1}, "norm2_apply": {-1: 0, 17: 1}, "x2_turn": {0: 0, 1: 1, 18: 2, 19: 3},
    "x2_turn_copy": {-2: 0, 1: 1, 19: 2, 20: 3}, "logits": {3: 0, 22: 1}, "route": {5: 0, 22: 1},
    "route_exp": {8: 0, 33: 1}, "route_weight": {14: 0, 41: 1},
}
SORT_WHOLE = {
    "rank": {23: 0}, "place": {25: 0}, "scatter": {26: 0, 29: 1}, "sorted_load": {32: 0, 33: 1, 34: 2, 42: 3},
    "sorted_turn": {34: 0, 36: 1, 38: 2, 39: 3, 41: 4, 43: 5, 46: 6, 47: 7},
    "sorted_turn_copy": {34: 0, 36: 1, 37: 2, 38: 3, 42: 4, 44: 5, 45: 6, 50: 7},
    "expert_id": {31: 0, 32: 1, 34: 2, 36: 3, 40: 4, 41: 5, 43: 6, 48: 7},
    "expert": {36: 0, 38: 1, 40: 2, 42: 3, 44: 4, 46: 5, 47: 6, 50: 7},
    "expert_copy": {38: 0, 40: 1, 41: 2, 44: 3, 46: 4, 47: 5, 49: 6, 51: 7},
    "sorted_store": {39: 0, 42: 1, 46: 2, 49: 3}, "gather": {50: 0, 54: 1}, "combine": {57: 0, 59: 1},
    "out_store": {61: 0, 68: 1},
}
SORT_FIRST = {
    "rank": {6: 0}, "place": {8: 0}, "scatter": {8: 0}, "sorted_load": {13: 0, 18: 1, 19: 2},
    "sorted_turn": {14: 0, 16: 1, 18: 2, 20: 3, 25: 4, 27: 5},
    "sorted_turn_copy": {14: 0, 18: 1, 19: 2, 23: 3, 26: 4, 28: 5},
    "expert_id": {10: 0, 17: 1, 19: 2, 21: 3, 24: 4, 26: 5}, "expert": {18: 0, 19: 1, 21: 2, 23: 3, 26: 4, 30: 5},
    "expert_copy": {19: 0, 20: 1, 22: 2, 24: 3, 26: 4, 27: 5}, "sorted_store": {20: 0, 28: 1, 31: 2},
    "gather": {34: 0}, "combine": {31: 0}, "out_store": {42: 0},
}
SORT_SECOND = {
    "rank": {24: 0}, "place": {22: 0}, "scatter": {30: 1}, "sorted_load": {30: 0, 34: 1, 35: 2},
    "sorted_turn": {34: 0, 39: 1, 41: 2, 43: 3, 45: 4, 47: 5},
    "sorted_turn_copy": {32: 0, 38: 1, 40: 2, 45: 3, 47: 4, 49: 5},
    "expert_id": {37: 0, 40: 1, 42: 2, 44: 3, 46: 4, 48: 5}, "expert": {40: 0, 42: 1, 43: 2, 45: 3, 47: 4, 49: 5},
    "expert_copy": {38: 0, 41: 1, 44: 2, 47: 3, 52: 4, 54: 5}, "sorted_store": {46: 0, 49: 1, 50: 2},
    "gather": {61: 1}, "combine": {58: 1}, "out_store": {66: 1},
}
WO_TURN = -2
EXPERT_LOAD = {-27: 0, 5: 1}
EXPERT_TURN = {1: 0, 3: 1, 5: 2, 4: 3, 11: 4, 12: 5, 13: 6, 14: 7}
BIAS_LOAD, BIAS_PARTS = -3, {9: 0, 14: 1, 20: 2}
ZERO_FILL = -3


def gated_block(nc, x, ctx, g_xattn, g_ffn, w_q, w_k, w_v, w_o, router_w, router_b, expert_w, expert_b, out,
                sorted_room, expert_room):
    B, S, D = x.shape
    KV = ctx.shape[1]
    E = router_w.shape[0]
    H = 16
    HD = D // H
    T = S // P
    C = D // P
    HPC = P // HD
    REM = KV - P
    KVP = P + 32
    HALF = 512
    NH = S // HALF
    TH = HALF // P
    SCALE = float(HD) ** -0.5
    PARTS = [(0, 0), (0, 1), (0, 2), (1, 0), (1, 1), (2, 0)]
    NP = len(PARTS)
    MROW = NP * HD
    KROWS = MROW + 1
    UNITS = [(hf, pr, par) for hf in range(NH) for pr in range(2) for par in range(2)]
    NU = len(UNITS)
    HEADS3 = [(0, 3), (3, 6), (6, 8)]
    GROUPS = [(b, 0, T, SORT_WHOLE, 0) for b in range(B - 1)] + [(B - 1, 0, TH, SORT_FIRST, 0),
                                                                 (B - 1, TH, T, SORT_SECOND, 1)]
    NG = len(GROUPS)
    TILES = [t1 - t0 + E - 1 for _, t0, t1, _, _ in GROUPS]
    ST = max(TILES)
    SC = 4
    CHUNKS = [[(i, min(i + 4, n)) for i in range(0, n, 4)] for n in TILES]
    PAIRS = [[(i, min(i + 2, n)) for i in range(0, n, 2)] for n in TILES]
    CHUNK0 = [sum(len(c) for c in CHUNKS[:g]) for g in range(NG)]
    PAIR0 = [sum(len(c) for c in PAIRS[:g]) for g in range(NG + 1)]
    CHUNK_OF = [(g, s) for g in range(NG) for s in range(len(CHUNKS[g]))]
    NC = max(len(c) for c in CHUNKS)
    RING = 3

    def chunk_count(g, s):
        return sum(len(CHUNKS[i]) > s for i in range(g + 1))

    def now_sort(name, g, step):
        return GROUPS[g][3][name].get(step - STEPS * (GROUPS[g][0] + 1))
    FIRST, LAST = -STEPS - 8, STEPS * (B + 1) + 64

    def now(table, name, b, step):
        if table is FRONT:
            if name in ("x_load", "ctx_load") and b == 0:
                return None
            return (FRONT_ALONE if b == 0 else FRONT)[name].get(step - STEPS * (b - 1))
        return (BACK_ALONE if b == B - 1 else BACK)[name].get(step - STEPS * (b + 1))

    def now_half(name, b, step, late):
        return (FRONT_ALONE if b == 0 else FRONT)[name].get(2 * (step - STEPS * (b - 1)) + late)

    front_use, back_use = {}, {}
    for i in range(3):
        front_use["weight", 0, i] = i
    for step in range(FIRST, LAST):
        for b in range(B):
            for name in ("ctx_turn", "keys", "values", "x_turn", "query", "rough", "max_turn"):
                i = now_half(name, b, step, 0) if name == "rough" else now(FRONT, name, b, step)
                if i is not None:
                    if name == "values":
                        front_use[name, b, 0] = len(front_use)
                        front_use[name, b, 1] = len(front_use)
                    else:
                        front_use[name, b, i] = len(front_use)
        if step == WO_TURN:
            for i in range(3, 6):
                front_use["weight", 0, i] = len(front_use)
        for b in range(B):
            i = now_half("rough", b, step, 1)
            if i is not None:
                front_use["rough", b, i] = len(front_use)
        e = EXPERT_TURN.get(step)
        if e is not None:
            back_use["weight", 0, e] = len(back_use)
        for b in range(B):
            for name in ("project", "x2_turn", "logits"):
                i = now(BACK, name, b, step)
                if i is not None:
                    back_use[name, b, i] = len(back_use)
        for g in range(NG):
            for name in ("rank", "expert"):
                i = now_sort(name, g, step)
                if i is not None:
                    back_use[name, g, i] = len(back_use)

    with ExitStack() as es:
        def sb(name, shape, dt=F32):
            return es.enter_context(nc.sbuf_tensor(name, shape, dt))

        def sem(name):
            return es.enter_context(nc.semaphore(name))

        probs = sb("probs", [P, 2, 5, HALF])
        shared_b = sb("shared_b", [P, 2 * T * D])
        wsb = shared_b[:, 0:4 * C * D].rearrange("p (e c d) -> p e c d", e=4, c=C)
        wop = shared_b[:, 4 * C * D:5 * C * D].rearrange("p (c d) -> p c d", c=C)
        x1 = shared_b[:, :].rearrange("p (a t d) -> p a t d", a=2, t=T)
        bias = shared_b[0:96 + 1, T * D:T * D + E * D]

        ident = sb("ident", [P, P])
        ones_e = sb("ones_e", [P, E])
        before_b = sb("before_b", [P, P], BF16)
        ones_b = sb("ones_b", [P, P], BF16)
        part_rows = sb("part_rows", [96 + 1, P], BF16)
        headmask = sb("headmask", [P, HPC], BF16)
        wT = sb("wT", [P, 4, C, D])
        ewT = sb("ewT", [P, E, C, D])
        rwT = sb("rwT", [P, C, E])
        rb = sb("rb", [P, E])
        eb = sb("eb", [96 + 1, E, D], BF16)
        rev = sb("rev", [P, E])
        tile_no = sb("tile_no", [P, ST])
        tile_rows = sb("tile_rows", [P, T])
        gates = sb("gates", [P, 2])
        tg = sb("tg", [P, 2])
        neg_half = sb("neg_half", [P, T])

        ctxA = sb("ctxA", [P, D])
        ctxB = sb("ctxB", [REM, D])
        ctxT = sb("ctxT", [P, C, KVP])
        ctxT_rem = sb("ctxT_rem", [P, C, 4, 32])
        kp = [sb(f"kp{i}", [P, C, KVP], BF16) for i in range(3)]
        rk = sb("rk", [P, C, KVP])
        kblock = sb("kblock", [P, C, HPC, KV], BF16)
        kstack = sb("kstack", [KROWS, 2, H, KVP], BF16)
        vals = sb("vals", [P, 2, 2, 2, 4, 32])
        vrem = sb("vrem", [P, 2, 2, 2, 4, 32])

        xn = sb("xn", [P, T, D])
        xnT = sb("xnT", [P, C, S])
        st6 = sb("st6", [P, 2, T, 6])
        mv = sb("mv", [P, 2, T, 2])
        ve = sb("ve", [P, 2, T])
        rs0 = sb("rs0", [P, 2, T])
        nt = sb("nt", [P, 2, T])
        rstd = sb("rstd", [P, 2, T])
        qp = [sb("qp0", [P, C, S], BF16), sb("qp1", [P, C, HALF], BF16), sb("qp2", [P, C, HALF], BF16)]
        rq = sb("rq", [P, 2, HALF])
        qstack = sb("qstack", [KROWS, H, S], BF16)
        mx = sb("mx", [P, T, H])
        nmT = sb("nmT", [H, S], BF16)
        pv = sb("pv", [P, 2, HALF])
        den_pack = sb("den_pack", [P, 2, HALF // 32])
        rec_pack = sb("rec_pack", [P, 2, HALF // 32])
        rec_row = sb("rec_row", [P, HALF])
        pvn = sb("pvn", [P, 2, HALF])
        attnT = sb("attnT", [P, 2, S])

        xn2 = sb("xn2", [P, T, D])
        x2T = sb("x2T", [P, C, HALF])
        rwsb = x2T[0:E, 1, 0:D]
        before, ones = x2T[:, 0, 0:P], x2T[:, 0, P:2 * P]
        lg = sb("lg", [P, T, E])
        lm = sb("lm", [P, T])
        eq = sb("eq", [P, T, E])
        oh = sb("oh", [P, T, E], BF16)
        ex = sb("ex", [P, T, E])
        wt = sb("wt", [P, 2, T])
        counts_e = sb("counts_e", [P, E])
        over = sb("over", [P, E, T])
        tiles_e = sb("tiles_e", [P, E])
        upto_e = sb("upto_e", [P, E])
        base_e = sb("base_e", [P, E])
        pos = sb("pos", [P, T, E])
        posf = sb("posf", [P, T])
        idx = sb("idx", [P, 2, T], I32)
        past = sb("past", [P, ST, E])
        tile_ef = sb("tile_ef", [P, ST])
        tile_e = sb("tile_e", [P, 2, ST], I32)
        xs = sb("xs", [P, RING * SC, D])
        xsT = sb("xsT", [P, 2, 2, D])
        ewsb = xs[:, 0:8, :].rearrange("p (e c) d -> p e c d", e=4)
        yg = xn

        bank = [es.enter_context(nc.psum_tensor(f"bank{i}", [P, 512], F32)) for i in range(8)]
        front_bank, back_bank, score_bank, weigh_bank, turn_bank = bank[0:2], bank[2:4], bank[4:6], bank[6], bank[7]

        front_full = [sem(f"front_full{i}") for i in range(2)]
        front_free = [sem(f"front_free{i}") for i in range(2)]
        back_full = [sem(f"back_full{i}") for i in range(2)]
        back_free = [sem(f"back_free{i}") for i in range(2)]
        score_full = [sem(f"score_full{i}") for i in range(2)]
        weigh_full = sem("weigh_full")
        weigh_free = sem("weigh_free")
        turn_full = sem("turn_full")
        weight_in = [sem(f"weight_in{i}") for i in range(4)]
        small_in = sem("small_in")
        experts_in = sem("experts_in")
        bias_in = sem("bias_in")
        bias_split = sem("bias_split")
        bias_left = sem("bias_left")
        ident_done = sem("ident_done")
        ctx_room = sem("ctx_room")
        stack_room = sem("stack_room")
        consts_done = sem("consts_done")
        headmask_done = sem("headmask_done")
        wop_half = sem("wop_half")
        tanh_done = sem("tanh_done")
        zeroed = sem("zeroed")
        ctx_in = sem("ctx_in")
        x_in = sem("x_in")
        residual_in = sem("residual_in")
        ctxT_done = sem("ctxT_done")
        k1_done = sem("k1_done")
        k_parts = sem("k_parts")
        kblock_done = sem("kblock_done")
        kstack_in = sem("kstack_in")
        v_done = sem("v_done")
        var1_done = sem("var1_done")
        pow1_done = sem("pow1_done")
        xn_done = sem("xn_done")
        xnT_done = sem("xnT_done")
        q1_done = sem("q1_done")
        rq_done = sem("rq_done")
        q2_done = sem("q2_done")
        q3_done = sem("q3_done")
        qstack_in = sem("qstack_in")
        nmT_done = sem("nmT_done")
        max_in = sem("max_in")
        probs_done = sem("probs_done")
        pv_out = sem("pv_out")
        den_in = sem("den_in")
        rec_done = sem("rec_done")
        rec_in = sem("rec_in")
        pvn_done = sem("pvn_done")
        attn_done = sem("attn_done")
        x1_done = sem("x1_done")
        var2_done = sem("var2_done")
        pow2_done = sem("pow2_done")
        xn2_done = sem("xn2_done")
        x2T_done = sem("x2T_done")
        shifted_done = sem("shifted_done")
        ex_done = sem("ex_done")
        oh_done = sem("oh_done")
        idx_done = sem("idx_done")
        scattered = [sem(f"scattered{s}") for s in range(2)]
        sorted_in = [sem(f"sorted_in{s}") for s in range(NC)]
        xsT_done = sem("xsT_done")
        ys_done = sem("ys_done")
        ys_stored = [sem(f"ys_stored{s}") for s in range(NC)]
        gathered = [sem(f"gathered{s}") for s in range(2)]
        out_done = sem("out_done")
        out_written = [sem(f"out_written{s}") for s in range(2)]
        dve_chain = sem("dve_chain")
        pool_chain = sem("pool_chain")

        block = es.enter_context(nc.Block())

        x_tiles = x.rearrange("b (p t) d -> b p t d", p=P)
        out_tiles = out.rearrange("b (p t) d -> b p t d", p=P)

        def slot(head):
            return head % HPC * C + head // HPC

        def part(i):
            return slice(i * HALF, (i + 1) * HALF)

        @block.sync
        def _(sp):
            sp.dma_start(ctxA[:, :], ctx[0, 0:P]).then_inc(ctx_in, 16)
            sp.dma_start(ctxB[:, :], ctx[0, P:KV]).then_inc(ctx_in, 16)
            for i, w in enumerate((w_k, w_v)):
                sp.dma_start(wsb[:, i], w.rearrange("(c p) d -> p c d", p=P)).then_inc(weight_in[i], 16)
            sp.dma_start(xn[:, :, :], x_tiles[0]).then_inc(x_in, 16)
            for i, w in enumerate((w_q, w_o), 2):
                sp.dma_start(wsb[:, i], w.rearrange("(c p) d -> p c d", p=P)).then_inc(weight_in[i], 16)
            sp.dma_start(rwsb[:, :], router_w).then_inc(small_in, 16)
            sp.dma_start(rb[:, :], router_b.rearrange("(a e) -> a e", a=1).broadcast_to([P, E])).then_inc(small_in, 16)
            sp.dma_start(gates[:, 0:1], g_xattn.rearrange("(a e) -> a e", a=1).broadcast_to([P, 1])).then_inc(small_in, 16)
            sp.dma_start(gates[:, 1:2], g_ffn.rearrange("(a e) -> a e", a=1).broadcast_to([P, 1])).then_inc(small_in, 16)

            for step in range(FIRST, LAST):
                r = EXPERT_LOAD.get(step)
                if r is not None:
                    if r == 1:
                        sp.wait_ge(back_free[0], 2)
                        sp.wait_ge(back_free[1], 2)
                    sp.dma_start(ewsb[:, :, :, :], expert_w[4 * r:4 * r + 4].rearrange("e (c p) d -> p e c d", p=P)
                                 ).then_inc(experts_in, 16)
                if step == BIAS_LOAD:
                    n = front_use["weight", 0, 3]
                    sp.wait_ge(front_free[n % 2], n // 2 + 1)
                    sp.dma_start(bias, expert_b.rearrange("(a e) d -> a (e d)", a=1).broadcast_to([96 + 1, E * D])
                                 ).then_inc(bias_in, 16)
                if step == ZERO_FILL:
                    sp.wait_ge(consts_done, 1)
                    for room in sorted_room:
                        sp.dma_start(room.rearrange("(s p) d -> p s d", p=P),
                                     rec_row[:, 0:D].unsqueeze(1).broadcast_to([P, room.shape[0] // P, D])
                                     ).then_inc(zeroed, 16)
                for b in range(B):
                    if now(FRONT, "ctx_load", b, step) is not None:
                        sp.wait_ge(ctxT_done, b)
                        sp.dma_start(ctxA[:, :], ctx[b, 0:P]).then_inc(ctx_in, 16)
                        sp.dma_start(ctxB[:, :], ctx[b, P:KV]).then_inc(ctx_in, 16)
                    if now(FRONT, "x_load", b, step) is not None:
                        sp.wait_ge(xnT_done, 4 * b)
                        sp.dma_start(xn[:, :, :], x_tiles[b]).then_inc(x_in, 16)
                    if now(FRONT, "kstack_load", b, step) is not None:
                        sp.wait_ge(k1_done, b + 1)
                        sp.wait_ge(k_parts, b + 1)
                        if b == 0:
                            sp.wait_ge(stack_room, 1)
                        if b >= 2:
                            sp.wait_ge(score_full[0], 20 * (b - 1))
                            sp.wait_ge(score_full[1], 20 * (b - 1))
                        for n, (_, k) in enumerate(PARTS):
                            sp.dma_start(kstack[n * HD:(n + 1) * HD, b % 2], kp[k][:, :, :]).then_inc(kstack_in, 16)
                    hf = now(FRONT, "qstack_load", b, step)
                    if hf is not None:
                        sp.wait_ge(q1_done, 4 * b + 2 * hf + 2)
                        sp.wait_ge(q2_done, 4 * b + 2 * hf + 2)
                        sp.wait_ge(q3_done, 4 * b + 2 * hf + 2)
                        if b >= 1:
                            sp.wait_ge(score_full[0], 20 * (b - 1) + 10 * hf + 10)
                            sp.wait_ge(score_full[1], 20 * (b - 1) + 10 * hf + 10)
                        for n, (q, _) in enumerate(PARTS):
                            sp.dma_start(qstack[n * HD:(n + 1) * HD, :, part(hf)],
                                         qp[q][:, :, part(hf if q == 0 else 0)]).then_inc(qstack_in, 16)
                    hf = now(FRONT, "max_load", b, step)
                    if hf is not None:
                        sp.wait_ge(nmT_done, NH * b + hf + 1)
                        if b >= 1:
                            sp.wait_ge(score_full[0], 20 * (b - 1) + 10 * hf + 10)
                            sp.wait_ge(score_full[1], 20 * (b - 1) + 10 * hf + 10)
                        sp.dma_start(qstack[MROW:MROW + 1, :, part(hf)], nmT[:, part(hf)]).then_inc(max_in, 16)
                for g in range(NU * B):
                    hf, pr, par = UNITS[g % NU]
                    row = 16 * (1 - par)
                    if step == 5 * g + UNIT["den_load"]:
                        sp.wait_ge(pv_out, g + 1)
                        if g >= 2:
                            sp.wait_ge(rec_done, g - 1)
                        sp.dma_start(den_pack[:, g % 2, :], pv[row:P:32, g % 2, :]).then_inc(den_in, 16)
                    if step == 5 * g + UNIT["rec_load"]:
                        sp.wait_ge(rec_done, g + 1)
                        if g >= 1:
                            sp.wait_ge(pvn_done, g)
                        else:
                            sp.wait_ge(zeroed, 32)
                        sp.dma_start(rec_row[row:P:32, :], rec_pack[:, g % 2, :]).then_inc(rec_in, 16)
                for b in range(B):
                    if now(BACK, "residual_load", b, step) is not None:
                        if b >= 2:
                            sp.wait_ge(out_done, T * (b - 1))
                        else:
                            n = front_use["weight", 0, 3]
                            sp.wait_ge(front_free[n % 2], n // 2 + 1)
                            if b == 1:
                                sp.wait_ge(bias_split, 3)
                        sp.dma_start(x1[:, b % 2], x_tiles[b]).then_inc(residual_in, 16)
                for g, (b, t0, t1, _, room) in enumerate(GROUPS):
                    s = now_sort("sorted_load", g, step)
                    if s is not None:
                        lo, hi = CHUNKS[g][s]
                        m = CHUNK0[g] + s
                        for hf in range(t0 // TH, t1 // TH):
                            sp.wait_ge(scattered[hf], 16 * TH * (b + 1))
                        if m >= RING:
                            before_g, before_s = CHUNK_OF[m - RING]
                            sp.wait_ge(ys_stored[before_s], 16 * chunk_count(before_g, before_s))
                        sp.dma_start(xs[:, m % RING * SC:m % RING * SC + hi - lo, :],
                                     sorted_room[room][lo * P:hi * P, :].rearrange("(t p) d -> p t d", p=P)
                                     ).then_inc(sorted_in[s], 16)
                    s = now_sort("sorted_store", g, step)
                    if s is not None:
                        lo, hi = CHUNKS[g][s]
                        m = CHUNK0[g] + s
                        sp.wait_ge(ys_done, PAIR0[g] + min(2 * s + 2, len(PAIRS[g])))
                        if b >= 1:
                            sp.wait_ge(gathered[0], 16 * TH * b)
                            sp.wait_ge(gathered[1], 16 * TH * b)
                        sp.dma_start(expert_room[room][lo * P:hi * P, :].rearrange("(t p) d -> p t d", p=P),
                                     xs[:, m % RING * SC:m % RING * SC + hi - lo, :]).then_inc(ys_stored[s], 16)
                    hf = now_sort("out_store", g, step)
                    if hf is not None:
                        ts = slice(hf * TH, (hf + 1) * TH)
                        sp.wait_ge(out_done, T * b + TH * (hf + 1))
                        sp.dma_start(out_tiles[b][:, ts, :], yg[:, ts, :]).then_inc(out_written[hf], 16)
            sp.wait_ge(out_written[0], 16 * B)
            sp.wait_ge(out_written[1], 16 * B)

        @block.tensor
        def _(pe):
            def front_begin(name, b, i):
                n = front_use[name, b, i]
                if n >= 2:
                    pe.wait_ge(front_free[n % 2], n // 2)
                return front_bank[n % 2], front_full[n % 2]

            def back_begin(name, b, i):
                n = back_use[name, b, i]
                if n >= 2:
                    pe.wait_ge(back_free[n % 2], n // 2)
                return back_bank[n % 2], back_full[n % 2]

            def rough(b, n):
                t, c = n // 6, n // 3 % 2
                lo, hi = HEADS3[n % 3]
                pe.wait_ge(kblock_done, b + 1)
                pe.wait_ge(q1_done, 4 * b + 2 * (t // TH) + c + 1)
                F, full = front_begin("rough", b, n)
                pe.matmul(F[:, 0:(hi - lo) * KV], qp[0][:, c, t * P:(t + 1) * P], kblock[:, c, lo:hi, :],
                          start=True, stop=True).then_inc(full, 1)

            def turn_weight(F, src):
                for kc in range(C):
                    for oc in range(C):
                        mm = pe.transpose(F[:, (kc * C + oc) * P:(kc * C + oc + 1) * P], src[:, oc, kc * P:(kc + 1) * P],
                                          ident[:, :])
                return mm

            own = {}

            pe.wait_ge(ident_done, 1)
            for i in range(3):
                pe.wait_ge(weight_in[i], 16)
                F, full = front_begin("weight", 0, i)
                turn_weight(F, wsb[:, i]).then_inc(full, 1)

            for step in range(FIRST, LAST):
                if 0 <= step < STEPS * B:
                    g, k = step // 5, step % 5
                    b, u = g // NU, g % NU
                    hf, pr, par = UNITS[u]
                    h0 = pr * 8 + par * 4
                    if k == 0:
                        if u == 0:
                            pe.wait_ge(kstack_in, 16 * NP * (b + 1))
                        if u % 4 == 0:
                            pe.wait_ge(qstack_in, 16 * NP * (NH * b + hf + 1))
                            pe.wait_ge(max_in, 16 * (NH * b + hf + 1))
                    if step >= 2:
                        pe.wait_ge(probs_done, step - 1)
                    sc = score_bank[step % 2]
                    if k < 4:
                        mm = pe.matmul(sc[:, :], kstack[:, b % 2, slot(h0 + k), 0:P], qstack[:, slot(h0 + k), part(hf)],
                                       start=True, stop=True)
                    else:
                        for j in range(4):
                            mm = pe.matmul(sc[32 * j:32 * j + 32, :], kstack[:, b % 2, slot(h0 + j), P:KVP],
                                           qstack[:, slot(h0 + j), part(hf)], start=True, stop=True)
                    mm.then_inc(score_full[step % 2], 1)

                for g in range(NU * B):
                    if step == 5 * g + UNIT["weigh"]:
                        b = g // NU
                        hf, pr, par = UNITS[g % NU]
                        o = weigh_bank
                        if g % NU == 0:
                            pe.wait_ge(v_done, b + 1)
                        if g >= 1:
                            pe.wait_ge(weigh_free, g)
                        pe.wait_ge(probs_done, 5 * g + 5)
                        for j in range(4):
                            pe.matmul(o[32 * j:32 * j + 32, :], vals[:, b % 2, pr, par, j, :], probs[:, g % 2, j, :],
                                      start=True, stop=False, skip_group_check=True)
                        pe.matmul(o[:, :], vrem[:, b % 2, pr, par, :, :], probs[:, g % 2, 4, :],
                                  start=False, stop=True, skip_group_check=True).then_inc(weigh_full, 1)

                for b in range(B):
                    if now(FRONT, "ctx_turn", b, step) is not None:
                        pe.wait_ge(ctx_in, 32 * (b + 1))
                        F, full = front_begin("ctx_turn", b, 0)
                        for kc in range(C):
                            pe.transpose(F[:, kc * KV:kc * KV + P], ctxA[:, kc * P:(kc + 1) * P], ident[:, :])
                            mm = pe.transpose(F[:, kc * KV + P:(kc + 1) * KV], ctxB[:, kc * P:(kc + 1) * P],
                                              ident[0:REM, 0:REM])
                        mm.then_inc(full, 1)
                    if now(FRONT, "keys", b, step) is not None:
                        pe.wait_ge(ctxT_done, b + 1)
                        if b == 0:
                            pe.wait_ge(front_free[0], 1)
                        F, full = front_begin("keys", b, 0)
                        for c in range(C):
                            for kc in range(C):
                                mm = pe.matmul(F[:, c * KVP:(c + 1) * KVP], wT[:, 0, kc, c * P:(c + 1) * P], ctxT[:, kc, :],
                                               start=kc == 0, stop=kc == C - 1)
                        mm.then_inc(full, 1)
                    if now(FRONT, "values", b, step) is not None:
                        if b == 0:
                            pe.wait_ge(front_free[1], 1)
                        F, full = front_begin("values", b, 0)
                        for kc in range(C):
                            mm = pe.matmul(F[:, 0:D], ctxT[:, kc, 0:P], wT[:, 1, kc, :], start=kc == 0, stop=kc == C - 1)
                        mm.then_inc(full, 1)
                        F, full = front_begin("values", b, 1)
                        for kc in range(C):
                            mm = pe.matmul(F[:, 0:D], ctxT_rem[:, kc].rearrange("p j k -> p (j k)"), wT[:, 1, kc, :],
                                           start=kc == 0, stop=kc == C - 1)
                        mm.then_inc(full, 1)
                    k = now(FRONT, "x_turn", b, step)
                    if k is not None:
                        hf, c = k // 2, k % 2
                        pe.wait_ge(xn_done, T * b + TH * (hf + 1))
                        F, full = front_begin("x_turn", b, k)
                        for t in range(TH):
                            mm = pe.transpose(F[:, t * P:(t + 1) * P], xn[:, hf * TH + t, c * P:(c + 1) * P], ident[:, :])
                        mm.then_inc(full, 1)
                    k = now(FRONT, "query", b, step)
                    if k is not None:
                        hf, c = k // 2, k % 2
                        pe.wait_ge(xnT_done, 4 * b + 2 * hf + 2)
                        if b == 0:
                            pe.wait_ge(front_free[0], 2)
                        F, full = front_begin("query", b, k)
                        for kc in range(C):
                            mm = pe.matmul(F[:, :], wT[:, 2, kc, c * P:(c + 1) * P], xnT[:, kc, part(hf)],
                                           start=kc == 0, stop=kc == C - 1)
                        mm.then_inc(full, 1)
                    n = now_half("rough", b, step, 0)
                    if n is not None:
                        rough(b, n)
                    hf = now(FRONT, "max_turn", b, step)
                    if hf is not None:
                        for n in (front_use["rough", b, 24 * hf + 23], front_use["rough", b, 24 * hf + 22]):
                            pe.wait_ge(front_free[n % 2], n // 2 + 1)
                        F, full = front_begin("max_turn", b, hf)
                        for t in range(TH):
                            mm = pe.transpose(F[0:H, t * P:(t + 1) * P], mx[:, hf * TH + t, :], ident[:, :])
                        mm.then_inc(full, 1)

                if step == WO_TURN:
                    pe.wait_ge(wop_half, 2)
                    F, full = front_begin("weight", 0, 3)
                    turn_weight(F, wop).then_inc(full, 1)
                    pe.wait_ge(small_in, 64)
                    for kc in range(C):
                        F, full = front_begin("weight", 0, 4 + kc)
                        pe.transpose(F[:, 0:E], rwsb[:, kc * P:(kc + 1) * P], ident[0:E, 0:E]).then_inc(full, 1)
                for b in range(B):
                    n = now_half("rough", b, step, 1)
                    if n is not None:
                        rough(b, n)

                e = EXPERT_TURN.get(step)
                if e is not None:
                    pe.wait_ge(experts_in, 16 * (e // 4 + 1))
                    F, full = back_begin("weight", 0, e)
                    turn_weight(F, ewsb[:, e % 4]).then_inc(full, 1)
                for b in range(B):
                    t = now(BACK, "project", b, step)
                    if t is not None:
                        pe.wait_ge(attn_done, 4 * b + 2 * (t // TH) + 2)
                        if b == 0 and t == 0:
                            for i in range(3, 6):
                                n = front_use["weight", 0, i]
                                pe.wait_ge(front_free[n % 2], n // 2 + 1)
                        F, full = back_begin("project", b, t)
                        for pr in range(2):
                            mm = pe.matmul(F[:, 0:D], attnT[:, pr, t * P:(t + 1) * P], wT[:, 3, pr, :],
                                           start=pr == 0, stop=pr == 1)
                        mm.then_inc(full, 1)
                    k = now(BACK, "x2_turn", b, step)
                    if k is not None:
                        pe.wait_ge(xn2_done, T * b + 2 * k + 2)
                        F, full = back_begin("x2_turn", b, k)
                        for c in range(C):
                            for t in range(2):
                                mm = pe.transpose(F[:, (c * 2 + t) * P:(c * 2 + t + 1) * P],
                                                  xn2[:, 2 * k + t, c * P:(c + 1) * P], ident[:, :])
                        mm.then_inc(full, 1)
                    hf = now(BACK, "logits", b, step)
                    if hf is not None:
                        pe.wait_ge(x2T_done, 4 * b + 2 * hf + 2)
                        F, full = back_begin("logits", b, hf)
                        for t in range(TH):
                            for kc in range(C):
                                mm = pe.matmul(F[:, t * E:(t + 1) * E], x2T[:, kc, t * P:(t + 1) * P], rwT[:, kc, :],
                                               start=kc == 0, stop=kc == C - 1)
                        mm.then_inc(full, 1)
                for g, (b, t0, t1, _, _) in enumerate(GROUPS):
                    if now_sort("rank", g, step) is not None:
                        n = t1 - t0
                        if g == 0:
                            pe.wait_ge(consts_done, 1)
                        pe.wait_ge(oh_done, NH * b + t1 // TH)
                        F, full = back_begin("rank", g, 0)
                        pe.matmul(F[:, 0:n * E], before_b[:, :], oh[:, t0:t1, :], start=True, stop=False,
                                  skip_group_check=True)
                        for s in range(1, n + 1):
                            mm = pe.matmul(F[:, s * E:(n + 1) * E], ones_b[:, :], oh[:, t0:t1 + 1 - s, :],
                                           start=False, stop=s == n, skip_group_check=True)
                        mm.then_inc(full, 1)
                    i = now_sort("sorted_turn", g, step)
                    if i is not None:
                        lo, hi = PAIRS[g][i]
                        s, m = lo // SC, CHUNK0[g] + lo // SC
                        pe.wait_ge(sorted_in[s], 16 * chunk_count(g, s))
                        if PAIR0[g] + i >= 1:
                            pe.wait_ge(xsT_done, PAIR0[g] + i)
                        for q in range(hi - lo):
                            for c in range(C):
                                mm = pe.transpose(turn_bank[:, (q * C + c) * P:(q * C + c + 1) * P],
                                                  xs[:, m % RING * SC + lo % SC + q, c * P:(c + 1) * P], ident[:, :])
                        mm.then_inc(turn_full, 1)
                    i = now_sort("expert_id", g, step)
                    if i is not None:
                        pe.wait_ge(idx_done, g + 1)
                        lo, hi = PAIRS[g][i]
                        own[g, i] = [pe.value_load(tile_e[0:1, g % 2, t:t + 1]) for t in range(lo, hi)]
                    i = now_sort("expert", g, step)
                    if i is not None:
                        pe.wait_ge(xsT_done, PAIR0[g] + i + 1)
                        if g == 0 and i == 0:
                            for e in range(E - 2, E):
                                n = back_use["weight", 0, e]
                                pe.wait_ge(back_free[n % 2], n // 2 + 1)
                            pe.wait_ge(bias_split, 3)
                        F, full = back_begin("expert", g, i)
                        for q, e in enumerate(own.pop((g, i))):
                            for kc in range(C):
                                pe.matmul(F[:, q * D:(q + 1) * D], xsT[:, i % 2, q, kc * P:(kc + 1) * P],
                                          ewT[:, bass.ds(e, 1), kc, :], start=kc == 0, stop=False)
                            mm = pe.matmul(F[:, q * D:(q + 1) * D], part_rows[:, :], eb[:, bass.ds(e, 1), :],
                                           start=False, stop=True)
                        mm.then_inc(full, 1)

        @block.scalar
        def _(act):
            def front_wait(name, b, i):
                n = front_use[name, b, i]
                act.wait_ge(front_full[n % 2], n // 2 + 1)
                return front_bank[n % 2], front_free[n % 2]

            def back_wait(name, b, i):
                n = back_use[name, b, i]
                act.wait_ge(back_full[n % 2], n // 2 + 1)
                return back_bank[n % 2], back_free[n % 2]

            for i in (0, 2):
                F, free = front_wait("weight", 0, i)
                act.copy(wT[:, i].rearrange("p c (g d h) -> p (c g) d h", h=HPC, d=HD),
                         F[:, :].rearrange("p (g h d) -> p g d h", h=HPC, d=HD)).then_inc(free, 1)
            act.wait_ge(small_in, 64)
            act.activation(tg[:, :], gates[:, :], ACT.Tanh).then_inc(tanh_done, 1)
            act.wait_ge(ctx_room, 1)
            act.wait_ge(stack_room, 1)

            for step in range(FIRST, LAST):
                if 0 <= step < STEPS * B:
                    g, k = step // 5, step % 5
                    if g >= 2:
                        act.wait_ge(weigh_full, g - 1)
                    act.wait_ge(score_full[step % 2], step // 2 + 1)
                    act.activation(probs[:, g % 2, k, :], score_bank[step % 2][:, :], ACT.Exp, scale=SCALE
                                   ).then_inc(probs_done, 1)
                for g in range(NU * B):
                    if step == 5 * g + UNIT["weigh_copy"]:
                        act.wait_ge(weigh_full, g + 1)
                        if g >= 2:
                            act.wait_ge(pvn_done, g - 1)
                            act.wait_ge(den_in, 16 * (g - 1))
                        act.copy(pv[:, g % 2, :], weigh_bank[:, :]).then_inc(pv_out, 1)
                        act.wait_ge(pv_out, g + 1)
                        act.sem_inc(weigh_free, 1)
                for b in range(B):
                    if now(FRONT, "ctx_copy", b, step) is not None:
                        F, free = front_wait("ctx_turn", b, 0)
                        if b >= 1:
                            n = front_use["values", b - 1, 1]
                            act.wait_ge(front_full[n % 2], n // 2 + 1)
                        Fc = F[:, 0:C * KV].rearrange("p (c k) -> p c k", c=C)
                        for j in range(4):
                            act.copy(ctxT_rem[:, :, j, 0:REM], Fc[:, :, P:KV])
                        act.copy(ctxT[:, :, 0:KV], Fc).then_inc(ctxT_done, 1)
                        act.wait_ge(ctxT_done, b + 1)
                        act.sem_inc(free, 1)
                    if now(FRONT, "key_parts", b, step) is not None:
                        F, free = front_wait("keys", b, 0)
                        if b >= 1:
                            act.wait_ge(kstack_in, 16 * NP * b)
                            act.wait_ge(kblock_done, b)
                        act.copy(kp[0][:, :, :].rearrange("p c k -> p (c k)"), F[:, 0:C * KVP]).then_inc(k1_done, 1)
                    if now(FRONT, "value_copy", b, step) is not None:
                        if b >= 2:
                            act.wait_ge(weigh_full, NU * (b - 1))
                        F, free = front_wait("values", b, 0)
                        for par in range(2):
                            ins = act.copy(vals[:, b % 2, :, par, :, 16 * par:16 * par + 16],
                                           F[:, 0:D].rearrange("p (r s j d) -> p r s j d", r=2, s=2, j=4)[:, :, par])
                        ins.then_inc(free, 1)
                        F, free = front_wait("values", b, 1)
                        for par in range(2):
                            for j in range(4):
                                q = slice(32 * j, 32 * j + 32)
                                ins = act.copy(vrem[q, b % 2, :, par, j, 16 * par:16 * par + 16],
                                               F[q, 0:D].rearrange("p (r s j d) -> p r s j d", r=2, s=2, j=4)[:, :, par, j])
                        ins.then_inc(v_done, 1)
                        act.wait_ge(v_done, b + 1)
                        act.sem_inc(free, 1)
                    k = now(FRONT, "x_turn_copy", b, step)
                    if k is not None:
                        hf, c = k // 2, k % 2
                        if b >= 1 and k == 0:
                            n = front_use["query", b - 1, 3]
                            act.wait_ge(front_full[n % 2], n // 2 + 1)
                        F, free = front_wait("x_turn", b, k)
                        act.copy(xnT[:, c, part(hf)], F[:, :]).then_inc(xnT_done, 1)
                        act.wait_ge(xnT_done, 4 * b + k + 1)
                        act.sem_inc(free, 1)
                    k = now(FRONT, "query_part1", b, step)
                    if k is not None:
                        hf, c = k // 2, k % 2
                        F, free = front_wait("query", b, k)
                        if b >= 1:
                            act.wait_ge(qstack_in, 16 * NP * (NH * (b - 1) + hf + 1))
                            n = front_use["rough", b - 1, 24 * hf + 23]
                            act.wait_ge(front_full[n % 2], n // 2 + 1)
                        act.copy(qp[0][:, c, part(hf)], F[:, :]).then_inc(q1_done, 1)
                    k = now(FRONT, "query_part2", b, step)
                    if k is not None:
                        hf, c = k // 2, k % 2
                        act.wait_ge(rq_done, 4 * b + k + 1)
                        if NH * b + hf >= 1:
                            act.wait_ge(qstack_in, 16 * NP * (NH * b + hf))
                        act.copy(qp[1][:, c, :], rq[:, k % 2, :]).then_inc(q2_done, 1)
                    hf = now(FRONT, "max_copy", b, step)
                    if hf is not None:
                        F, free = front_wait("max_turn", b, hf)
                        if b >= 1:
                            act.wait_ge(max_in, 16 * (NH * (b - 1) + hf + 1))
                        act.mul(nmT[:, part(hf)], F[0:H, :], -1.0).then_inc(nmT_done, 1)
                        act.wait_ge(nmT_done, NH * b + hf + 1)
                        act.sem_inc(free, 1)
                if step == WO_TURN + 1:
                    act.wait_ge(consts_done, 1)
                    F, free = front_wait("weight", 0, 4)
                    act.copy(rwT[:, 0, :], F[:, 0:E]).then_inc(free, 1)
                e = EXPERT_TURN.get(step - 1)
                if e is not None and e % 2 == 0:
                    F, free = back_wait("weight", 0, e)
                    act.copy(ewT[:, e].rearrange("p c d -> p (c d)"), F[:, :]).then_inc(free, 1)
                i = BIAS_PARTS.get(step)
                if i is not None:
                    at = (0, 64, 96)[i]
                    act.wait_ge(bias_in, 16)
                    if i >= 1:
                        act.wait_ge(bias_left, i)
                    act.copy(eb[at:96 + 1, :, :].rearrange("p e d -> p (e d)"), bias[at:96 + 1, :]
                             ).then_inc(bias_split, 1)
                for b in range(B):
                    k = now(BACK, "x2_turn_copy", b, step)
                    if k is not None:
                        F, free = back_wait("x2_turn", b, k)
                        if k % 2 == 0 and 2 * b + k // 2 >= 1:
                            n = back_use["logits", b, 0] if k == 2 else back_use["logits", b - 1, 1]
                            act.wait_ge(back_full[n % 2], n // 2 + 1)
                        act.copy(x2T[:, :, (k % 2) * 2 * P:(k % 2 + 1) * 2 * P],
                                 F[:, :].rearrange("p (c k) -> p c k", c=C)).then_inc(x2T_done, 1)
                        act.wait_ge(x2T_done, 4 * b + k + 1)
                        act.sem_inc(free, 1)
                    hf = now(BACK, "route_exp", b, step)
                    if hf is not None:
                        act.wait_ge(shifted_done, NH * b + hf + 1)
                        ts = slice(hf * TH, (hf + 1) * TH)
                        act.activation(ex[:, ts, :], ex[:, ts, :], ACT.Exp).then_inc(ex_done, 1)
                for g in range(NG):
                    i = now_sort("sorted_turn_copy", g, step)
                    if i is not None:
                        lo, hi = PAIRS[g][i]
                        if PAIR0[g] + i >= 2:
                            h = g if i >= 2 else g - 1
                            n = back_use["expert", h, PAIR0[g] + i - 2 - PAIR0[h]]
                            act.wait_ge(back_full[n % 2], n // 2 + 1)
                        act.wait_ge(turn_full, PAIR0[g] + i + 1)
                        act.copy(xsT[:, i % 2, 0:hi - lo, :].rearrange("p q d -> p (q d)"), turn_bank[:, 0:(hi - lo) * D]
                                 ).then_inc(xsT_done, 1)

        @block.vector
        def _(dve):
            done = [0]

            def link(ins):
                done[0] += 1
                ins.then_inc(dve_chain, 1)
                dve.wait_ge(dve_chain, done[0])

            def front_wait(name, b, i):
                n = front_use[name, b, i]
                dve.wait_ge(front_full[n % 2], n // 2 + 1)
                return front_bank[n % 2], front_free[n % 2]

            def back_wait(name, b, i):
                n = back_use[name, b, i]
                dve.wait_ge(back_full[n % 2], n // 2 + 1)
                return back_bank[n % 2], back_free[n % 2]

            def stats(which, src, hf, var_done):
                ts = range(hf * TH, (hf + 1) * TH)
                for t in ts:
                    ins = dve.bn_stats(st6[:, which, t, :], src[:, t, :])
                link(ins)
                for t in ts:
                    ins = dve.bn_aggr(mv[:, which, t, :], st6[:, which, t, :])
                link(ins)
                dve.tensor_scalar(ve[:, which, ts[0]:ts[-1] + 1], mv[:, which, ts[0]:ts[-1] + 1, 1], EPS, None,
                                  ALU.add).then_inc(var_done, 1)

            def normalise(which, src, dst, hf, rows_done):
                ts = slice(hf * TH, (hf + 1) * TH)
                link(dve.tensor_tensor(nt[:, which, ts], rs0[:, which, ts], rs0[:, which, ts], ALU.mult))
                link(dve.tensor_tensor(nt[:, which, ts], nt[:, which, ts], ve[:, which, ts], ALU.mult))
                link(dve.tensor_scalar(nt[:, which, ts], nt[:, which, ts], -0.5, 1.5, ALU.mult, ALU.add))
                link(dve.tensor_tensor(rstd[:, which, ts], nt[:, which, ts], rs0[:, which, ts], ALU.mult))
                for t in range(hf * TH, (hf + 1) * TH):
                    dve.tensor_scalar(dst[:, t, :], src[:, t, :], mv[:, which, t, 0:1], rstd[:, which, t:t + 1],
                                      ALU.subtract, ALU.mult).then_inc(rows_done, 1)

            dve.wait_ge(ident_done, 1)
            dve.tensor_reduce(headmask[:, :], ident[:, :].rearrange("p (d h) -> p h d", h=HPC), AX_X,
                              ALU.max).then_inc(headmask_done, 1)
            dve.wait_ge(headmask_done, 1)
            F, free = front_wait("weight", 0, 1)
            dve.tensor_copy(wT[:, 1].rearrange("p c d -> p (c d)"), F[:, :]).then_inc(free, 1)

            def maxima(b, n):
                t, c = n // 6, n // 3 % 2
                lo, hi = HEADS3[n % 3]
                if b >= 1 and n % 24 == 0:
                    m = front_use["max_turn", b - 1, n // 24]
                    dve.wait_ge(front_full[m % 2], m // 2 + 1)
                F, free = front_wait("rough", b, n)
                dve.tensor_reduce(mx[:, t, :].rearrange("p (h c) -> p h c", c=C)[:, lo:hi, c],
                                  F[:, 0:(hi - lo) * KV].rearrange("p (h k) -> p h k", k=KV),
                                  AX_X, ALU.max).then_inc(free, 1)

            for step in range(FIRST, LAST):
                for b in range(B):
                    n = now_half("maxima", b, step, 0)
                    if n is not None:
                        maxima(b, n)
                for g in range(NG):
                    i = now_sort("expert_copy", g, step)
                    if i is not None:
                        lo, hi = PAIRS[g][i]
                        r = (CHUNK0[g] + lo // SC) % RING * SC + lo % SC
                        F, free = back_wait("expert", g, i)
                        dve.tensor_copy(xs[:, r:r + hi - lo, :].rearrange("p q d -> p (q d)"), F[:, 0:(hi - lo) * D]
                                        ).then_inc(ys_done, 1)
                        dve.wait_ge(ys_done, PAIR0[g] + i + 1)
                        dve.sem_inc(free, 1)
                for b in range(B):
                    if now(FRONT, "key_parts", b, step) is not None:
                        F, free = front_wait("keys", b, 0)
                        dve.wait_ge(k1_done, b + 1)
                        link(dve.tensor_tensor(rk[:, :, :].rearrange("p c k -> p (c k)"), F[:, 0:C * KVP],
                                               kp[0][:, :, :].rearrange("p c k -> p (c k)"), ALU.subtract))
                        dve.sem_inc(free, 1)
                        link(dve.tensor_copy(kp[1][:, :, :], rk[:, :, :]))
                        dve.tensor_tensor(kp[2][:, :, :], rk[:, :, :], kp[1][:, :, :], ALU.subtract).then_inc(k_parts, 1)
                        if b >= 1:
                            n = front_use["rough", b - 1, 47]
                            dve.wait_ge(front_full[n % 2], n // 2 + 1)
                        for c in range(C):
                            ins = dve.tensor_tensor(kblock[:, c], kp[0][:, c:c + 1, 0:KV].broadcast_to([P, HPC, KV]),
                                                    headmask[:, :].unsqueeze(2).broadcast_to([P, HPC, KV]), ALU.mult)
                        ins.then_inc(kblock_done, 1)
                    hf = now(FRONT, "norm1_stats", b, step)
                    if hf is not None:
                        dve.wait_ge(x_in, 16 * (b + 1))
                        stats(0, xn, hf, var1_done)
                    hf = now(FRONT, "norm1_apply", b, step)
                    if hf is not None:
                        dve.wait_ge(pow1_done, NH * b + hf + 1)
                        normalise(0, xn, xn, hf, xn_done)
                    k = now(FRONT, "query_rest", b, step)
                    if k is not None:
                        hf, c = k // 2, k % 2
                        F, free = front_wait("query", b, k)
                        dve.wait_ge(q1_done, 4 * b + k + 1)
                        if 4 * b + k >= 2:
                            dve.wait_ge(q2_done, 4 * b + k - 1)
                            dve.wait_ge(q3_done, 4 * b + k - 1)
                        dve.tensor_tensor(rq[:, k % 2, :], F[:, :], qp[0][:, c, part(hf)], ALU.subtract
                                          ).then_inc(rq_done, 1)
                        dve.wait_ge(rq_done, 4 * b + k + 1)
                        dve.sem_inc(free, 1)
                if step == WO_TURN - 2:
                    dve.wait_ge(weight_in[3], 16)
                    for par in range(2):
                        dve.tensor_copy(wop[:, :, :].rearrange("p c (r j s d) -> p (c r) j s d", r=2, s=2, j=4)[:, :, :, par],
                                        wsb[:, 3].rearrange("p c (r s j d) -> p (c r) s j d", r=2, s=2, j=4)[:, :, par]
                                        ).then_inc(wop_half, 1)
                if step == WO_TURN + 1:
                    dve.wait_ge(tanh_done, 1)
                    F, free = front_wait("weight", 0, 3)
                    dve.tensor_scalar(wT[:, 3].rearrange("p c d -> p (c d)"), F[:, :], tg[:, 0:1], None, ALU.mult
                                      ).then_inc(free, 1)
                    F, free = front_wait("weight", 0, 5)
                    dve.tensor_copy(rwT[:, 1, :], F[:, 0:E]).then_inc(free, 1)
                    dve.wait_ge(consts_done, 1)
                e = EXPERT_TURN.get(step - 1)
                if e is not None and e % 2 == 1:
                    F, free = back_wait("weight", 0, e)
                    dve.tensor_copy(ewT[:, e].rearrange("p c d -> p (c d)"), F[:, :]).then_inc(free, 1)
                i = BIAS_PARTS.get(step - 1)
                if i is not None and i < 2:
                    dve.wait_ge(bias_split, i + 1)
                    q = slice((64, 96)[i], 96 + 1)
                    dve.tensor_tensor(bias[q, :], bias[q, :], eb[q, :, :].rearrange("p e d -> p (e d)"), ALU.subtract
                                      ).then_inc(bias_left, 1)
                for g in range(NU * B):
                    hf, pr, par = UNITS[g % NU]
                    if step == 5 * g + UNIT["den_recip"]:
                        dve.wait_ge(den_in, 16 * (g + 1))
                        if g >= 2:
                            dve.wait_ge(rec_in, 16 * (g - 1))
                        dve.reciprocal(rec_pack[:, g % 2, :], den_pack[:, g % 2, :]).then_inc(rec_done, 1)
                    if step == 5 * g + UNIT["normalise"]:
                        row, zero = 16 * (1 - par), 8
                        mask = ([row] * 16 + [zero] * 16) if par == 0 else ([zero] * 16 + [row] * 16)
                        dve.wait_ge(rec_in, 16 * (g + 1))
                        if g >= 2:
                            dve.wait_ge(attn_done, g // 2)
                        link(dve.stream_shuffle(pvn[:, g % 2, :], rec_row[:, :], mask))
                        dve.tensor_tensor(pvn[:, g % 2, :], pv[:, g % 2, :], pvn[:, g % 2, :], ALU.mult).then_inc(pvn_done, 1)
                for b in range(B):
                    t = now(BACK, "residual", b, step)
                    if t is not None:
                        if t == 0:
                            dve.wait_ge(residual_in, 16 * (b + 1))
                        F, free = back_wait("project", b, t)
                        dve.tensor_tensor(x1[:, b % 2, t, :], F[:, 0:D], x1[:, b % 2, t, :], ALU.add).then_inc(x1_done, 1)
                        dve.wait_ge(x1_done, T * b + t + 1)
                        dve.sem_inc(free, 1)
                    hf = now(BACK, "norm2_stats", b, step)
                    if hf is not None:
                        stats(1, x1[:, b % 2], hf, var2_done)
                    hf = now(BACK, "norm2_apply", b, step)
                    if hf is not None:
                        dve.wait_ge(pow2_done, NH * b + hf + 1)
                        if b >= 1:
                            dve.wait_ge(scattered[0], 16 * TH * b)
                            dve.wait_ge(scattered[1], 16 * TH * b)
                        normalise(1, x1[:, b % 2], xn2, hf, xn2_done)
                    hf = now(BACK, "route", b, step)
                    if hf is not None:
                        ts = slice(hf * TH, (hf + 1) * TH)
                        full3 = [P, TH, E]
                        F, free = back_wait("logits", b, hf)
                        link(dve.tensor_tensor(lg[:, ts, :], F[:, 0:TH * E].rearrange("p (t e) -> p t e", e=E),
                                               rb[:, :].unsqueeze(1).broadcast_to(full3), ALU.add))
                        dve.sem_inc(free, 1)
                        link(dve.tensor_reduce(lm[:, ts], lg[:, ts, :], AX_X, ALU.max))
                        top = lm[:, ts].unsqueeze(2).broadcast_to(full3)
                        dve.tensor_tensor(ex[:, ts, :], lg[:, ts, :], top, ALU.subtract).then_inc(shifted_done, 1)
                        link(dve.tensor_tensor(eq[:, ts, :], lg[:, ts, :], top, ALU.is_equal))
                        link(dve.tensor_tensor(eq[:, ts, :], eq[:, ts, :], rev[:, :].unsqueeze(1).broadcast_to(full3), ALU.mult))
                        link(dve.tensor_reduce(lm[:, ts], eq[:, ts, :], AX_X, ALU.max))
                        dve.tensor_tensor(oh[:, ts, :], eq[:, ts, :], top, ALU.is_equal).then_inc(oh_done, 1)
                    hf = now(BACK, "route_weight", b, step)
                    if hf is not None:
                        ts = slice(hf * TH, (hf + 1) * TH)
                        w = wt[:, b % 2, ts]
                        dve.wait_ge(ex_done, NH * b + hf + 1)
                        link(dve.tensor_reduce(w, ex[:, ts, :], AX_X, ALU.add))
                        link(dve.reciprocal(w, w))
                        link(dve.tensor_scalar(w, w, tg[:, 1:2], None, ALU.mult))
                for g, (b, t0, t1, _, room) in enumerate(GROUPS):
                    if now_sort("place", g, step) is not None:
                        n, tiles = t1 - t0, TILES[g]
                        F, free = back_wait("rank", g, 0)
                        if b >= 2:
                            dve.wait_ge(gathered[0], 16 * TH * (b - 1))
                            dve.wait_ge(gathered[1], 16 * TH * (b - 1))
                        if g >= 2:
                            u = back_use["expert", g - 2, len(PAIRS[g - 2]) - 1]
                            dve.wait_ge(back_full[u % 2], u // 2 + 1)
                        link(dve.tensor_copy(counts_e[:, :], F[:, n * E:(n + 1) * E]))
                        link(dve.tensor_tensor(over[:, :, 0:n], counts_e[:, :].unsqueeze(2).broadcast_to([P, E, n]),
                                               tile_rows[:, 0:n].unsqueeze(1).broadcast_to([P, E, n]), ALU.is_gt))
                        link(dve.tensor_reduce(tiles_e[:, :], over[:, :, 0:n], AX_X, ALU.add))
                        link(dve.tensor_tensor_scan(upto_e[:, :], ones_e[:, :], tiles_e[:, :], 0.0, ALU.mult, ALU.add))
                        link(dve.tensor_tensor(base_e[:, :], upto_e[:, :], tiles_e[:, :], ALU.subtract))
                        link(dve.tensor_scalar(base_e[:, :], base_e[:, :], float(P), None, ALU.mult))
                        link(dve.tensor_tensor(pos[:, 0:n, :], F[:, 0:n * E].rearrange("p (t e) -> p t e", e=E),
                                               base_e[:, :].unsqueeze(1).broadcast_to([P, n, E]), ALU.add))
                        dve.sem_inc(free, 1)
                        link(dve.tensor_tensor(pos[:, 0:n, :], pos[:, 0:n, :], oh[:, t0:t1, :], ALU.mult))
                        link(dve.tensor_reduce(posf[:, 0:n], pos[:, 0:n, :], AX_X, ALU.add))
                        link(dve.tensor_copy(idx[:, b % 2, t0:t1], posf[:, 0:n]))
                        link(dve.tensor_tensor(past[:, 0:tiles, :], upto_e[:, :].unsqueeze(1).broadcast_to([P, tiles, E]),
                                               tile_no[:, 0:tiles].unsqueeze(2).broadcast_to([P, tiles, E]), ALU.is_le))
                        link(dve.tensor_reduce(tile_ef[:, 0:tiles], past[:, 0:tiles, :], AX_X, ALU.add))
                        link(dve.tensor_scalar(tile_ef[:, 0:tiles], tile_ef[:, 0:tiles], float(E - 1), None, ALU.min))
                        dve.tensor_copy(tile_e[:, g % 2, 0:tiles], tile_ef[:, 0:tiles]).then_inc(idx_done, 1)
                    hf = now_sort("combine", g, step)
                    if hf is not None:
                        dve.wait_ge(gathered[hf], 16 * TH * (b + 1))
                        for t in range(hf * TH, (hf + 1) * TH):
                            dve.scalar_tensor_tensor(yg[:, t, :], yg[:, t, :], wt[:, b % 2, t:t + 1], x1[:, b % 2, t, :],
                                                     ALU.mult, ALU.add).then_inc(out_done, 1)
                for b in range(B):
                    n = now_half("maxima", b, step, 1)
                    if n is not None:
                        maxima(b, n)

        @block.gpsimd
        def _(pool):
            done = [0]

            def link(ins):
                done[0] += 1
                ins.then_inc(pool_chain, 1)
                pool.wait_ge(pool_chain, done[0])

            link(pool.memset(ident[:, :], 0.0))
            pool.affine_select(out=ident[:, :], in_=ident[:, :], compare_op=ALU.not_equal, fill=1.0, base=0,
                               pattern=[[-1, P]], channel_multiplier=1).then_inc(ident_done, 1)
            pool.memset(neg_half[:, :], -0.5)
            pool.memset(ctxT[:, :, :], 0.0)
            pool.memset(ctxT_rem[:, :, :, :], 0.0).then_inc(ctx_room, 1)
            pool.memset(vals[:, :, :, :, :, :], 0.0)
            link(pool.memset(vrem[:, :, :, :, :, :], 0.0))
            for par in range(2):
                col = 16 * (1 - par)
                link(pool.memset(vals[:, :, :, par, :, col:col + 1], 1.0))
                for j in range(4):
                    link(pool.memset(vrem[32 * j:32 * j + REM, :, :, par, j, col:col + 1], 1.0))
            link(pool.memset(kstack[:, :, :, P:KVP], 0.0))
            link(pool.memset(kstack[MROW:MROW + 1, :, :, 0:KV], 1.0))
            pool.sem_inc(stack_room, 1)

            def consts():
                link(pool.memset(ones[:, :], 1.0))
                link(pool.affine_select(out=before[:, :], in_=ones[:, :], compare_op=ALU.is_gt, fill=0.0, base=0,
                                        pattern=[[1, P]], channel_multiplier=-1))
                pool.tensor_copy(before_b[:, :], before[:, :])
                pool.tensor_copy(ones_b[:, :], ones[:, :])
                link(pool.memset(part_rows[:, :], 0.0))
                for at in (0, 64, 96):
                    link(pool.memset(part_rows[at:at + 1, :], 1.0))
                pool.memset(ones_e[:, :], 1.0)
                for e in range(E):
                    pool.memset(rev[:, e:e + 1], float(E - e))
                for s in range(ST):
                    pool.memset(tile_no[:, s:s + 1], float(s))
                for t in range(T):
                    pool.memset(tile_rows[:, t:t + 1], float(P * t))
                link(pool.memset(rec_row[:, :], 0.0))
                pool.sem_inc(consts_done, 1)

            for step in range(FIRST, LAST):
                if step == -10:
                    consts()
                for b in range(B):
                    hf = now(FRONT, "norm1_power", b, step)
                    if hf is not None:
                        ts = slice(hf * TH, (hf + 1) * TH)
                        pool.wait_ge(var1_done, NH * b + hf + 1)
                        pool.tensor_tensor(rs0[:, 0, ts], ve[:, 0, ts], neg_half[:, ts], ALU.pow).then_inc(pow1_done, 1)
                    k = now(FRONT, "query_part3", b, step)
                    if k is not None:
                        hf, c = k // 2, k % 2
                        pool.wait_ge(q2_done, 4 * b + k + 1)
                        if NH * b + hf >= 1:
                            pool.wait_ge(qstack_in, 16 * NP * (NH * b + hf))
                        pool.tensor_tensor(qp[2][:, c, :], rq[:, k % 2, :], qp[1][:, c, :],
                                           ALU.subtract).then_inc(q3_done, 1)
                for g in range(1, NU * B, 2):
                    if step == 5 * g + UNIT["join"]:
                        b = g // NU
                        hf, pr, par = UNITS[g % NU]
                        pool.wait_ge(pvn_done, g + 1)
                        if b >= 1:
                            pool.wait_ge(x1_done, T * (b - 1) + TH * (hf + 1))
                        pool.tensor_tensor(attnT[:, pr, part(hf)], pvn[:, 0, :], pvn[:, 1, :], ALU.add).then_inc(attn_done, 1)
                for b in range(B):
                    hf = now(BACK, "norm2_power", b, step)
                    if hf is not None:
                        ts = slice(hf * TH, (hf + 1) * TH)
                        pool.wait_ge(var2_done, NH * b + hf + 1)
                        pool.tensor_tensor(rs0[:, 1, ts], ve[:, 1, ts], neg_half[:, ts], ALU.pow).then_inc(pow2_done, 1)
                for g, (b, t0, t1, _, room) in enumerate(GROUPS):
                    hf = now_sort("scatter", g, step)
                    if hf is not None:
                        if hf * TH == t0:
                            pool.wait_ge(idx_done, g + 1)
                            pool.wait_ge(xn2_done, T * b + t1)
                            if g == 0:
                                pool.wait_ge(zeroed, 32)
                            elif t0 == 0:
                                for s in range(len(CHUNKS[g - 1])):
                                    pool.wait_ge(sorted_in[s], 16 * chunk_count(g - 1, s))
                        for t in range(hf * TH, (hf + 1) * TH):
                            pool.indirect_dma_start(out=sorted_room[room],
                                                    out_offset=bass.IndirectOffsetOnAxis(ap=idx[:, b % 2, t:t + 1], axis=0),
                                                    in_=xn2[:, t, :], in_offset=None).then_inc(scattered[hf], 16)
                    hf = now_sort("gather", g, step)
                    if hf is not None:
                        if hf * TH == t0:
                            for s in range(len(CHUNKS[g])):
                                pool.wait_ge(ys_stored[s], 16 * chunk_count(g, s))
                            pool.wait_ge(xnT_done, 4 * min(b + 4, B))
                        if b >= 1:
                            pool.wait_ge(out_written[hf], 16 * b)
                        for t in range(hf * TH, (hf + 1) * TH):
                            pool.indirect_dma_start(out=yg[:, t, :], out_offset=None, in_=expert_room[room],
                                                    in_offset=bass.IndirectOffsetOnAxis(ap=idx[:, b % 2, t:t + 1], axis=0)
                                                    ).then_inc(gathered[hf], 16)


_INS = ["x", "ctx_1024", "g_xattn", "g_ffn", "L0_xattn_w_q", "L0_xattn_w_k", "L0_xattn_w_v", "L0_xattn_w_o",
        "L0_ffn_router_w", "L0_ffn_router_b", "L0_ffn_expert_w", "L0_ffn_expert_b"]


def kernel(**inputs):
    import numpy as _np
    import concourse.bacc as _bacc
    from concourse import mybir as _mybir
    from concourse.bass_utils import run_bass_kernel_spmd as _run

    nc = _bacc.Bacc("TRN2", target_bir_lowering=False, num_devices=1)
    arrays, args = {}, []
    for name in _INS:
        a = _np.ascontiguousarray(inputs[name])
        arrays[f"in_{name}"] = a
        args.append(nc.dram_tensor(f"in_{name}", a.shape, _mybir.dt.from_np(a.dtype), kind="ExternalInput").ap())
    _, s, d = inputs["x"].shape
    pad = (inputs["L0_ffn_router_w"].shape[0] - 1) * 128
    args.append(nc.dram_tensor("out_0", inputs["x"].shape, _mybir.dt.float32, kind="ExternalOutput").ap())
    for name in ("sorted_rows", "expert_rows"):
        args.append([nc.dram_tensor(name, (s + pad, d), _mybir.dt.float32).ap(),
                     nc.dram_tensor(name + "_half", (s // 2 + pad, d), _mybir.dt.float32).ap()])
    gated_block(nc, *args)
    r = _run(nc, [arrays], core_ids=[0])
    return r.results[0]["out_0"]
```
